# Optimizing a Trainium2 kernel written in Bass

```python
import numpy as np
import jax
import jax.numpy as jnp

def _softmax(x, axis=-1):
    return jax.nn.softmax(x, axis=axis)

def _gelu(x):
    return jax.nn.gelu(x, approximate=True)

def _silu(x):
    return jax.nn.silu(x)

def _sigmoid(x):
    return jax.nn.sigmoid(x)

def _layernorm(x, axis=-1, eps=1e-05):
    m = jnp.mean(x, axis=axis, keepdims=True)
    v = jnp.var(x, axis=axis, keepdims=True)
    return (x - m) / jnp.sqrt(v + eps)

def _scatter_add(tgt, idx, src, axis=0):
    return tgt.at[idx].add(src)

def _segment_sum(src, seg, n):
    return jax.ops.segment_sum(src, seg, n)
kernel_name = 'mk_macaron_d1_jaxref_r8_79a39f'

def setup_inputs(seed: int=0):
    np.random.seed(seed)
    _w = jnp.asarray

    def _L0_attn_setup():
        import math
        import jax, jax.numpy as jnp
        import numpy as np
        B, S, D, H, DH = (2, 256, 256, 16, 128)

        def _alibi_slopes(n):

            def pow2(m):
                start = 2 ** (-2 ** (-(math.log2(m) - 3)))
                return [start * start ** i for i in range(m)]
            if math.log2(n).is_integer():
                return pow2(n)
            c = 2 ** math.floor(math.log2(n))
            return pow2(c) + _alibi_slopes(2 * c)[0::2][:n - c]

        def _alibi_mask(n_heads, q_len, kv_len):
            slopes = jnp.asarray(np.array(_alibi_slopes(n_heads), dtype=np.float32))
            bias = slopes[:, None, None] * jnp.arange(kv_len, dtype=jnp.float32)[None, None, :]
            i = jnp.arange(q_len)[:, None]
            j = jnp.arange(kv_len)[None, :]
            causal = jnp.where(j > i, -jnp.inf, 0.0).astype(jnp.float32)
            return causal[None, :, :] + bias
        key = jax.random.key(seed)
        k1, k2, k3, k4, k5 = jax.random.split(key, 5)
        scale = 1.0 / math.sqrt(D)
        return {'resid_pre': jax.random.normal(k1, (B, S, D), dtype=jnp.float32), 'Wq': jax.random.normal(k2, (H * DH, D), dtype=jnp.float32) * scale, 'Wk': jax.random.normal(k3, (H * DH, D), dtype=jnp.float32) * scale, 'Wv': jax.random.normal(k4, (H * DH, D), dtype=jnp.float32) * scale, 'Wo': jax.random.normal(k5, (D, H * DH), dtype=jnp.float32) * scale}
    _L0_attn_in = _L0_attn_setup()

    def _L0_ffn_setup():
        import jax, jax.numpy as jnp
        import numpy as np
        HIDDEN = 256
        INTER = 1024
        SCALE = 64.0

        def fwht(x):
            orig_shape = x.shape
            n = orig_shape[-1]
            x = x.reshape(-1, n)
            h = 1
            while h < n:
                x = x.reshape(-1, n // (2 * h), 2, h)
                a, b = (x[:, :, 0, :], x[:, :, 1, :])
                x = jnp.stack([a + b, a - b], axis=2).reshape(-1, n)
                h *= 2
            return (x / jnp.sqrt(jnp.asarray(n, x.dtype))).reshape(orig_shape)
        key = jax.random.key(seed)
        ks = jax.random.split(key, 8)
        inp = jax.random.normal(ks[0], (4, 256, HIDDEN), dtype=jnp.float32)
        SU_ug = jnp.where(jax.random.bernoulli(ks[1], 0.5, (HIDDEN,)), 1.0, -1.0).astype(jnp.float32)
        SU_dp = jnp.where(jax.random.bernoulli(ks[2], 0.5, (INTER,)), 1.0, -1.0).astype(jnp.float32)
        Wscale_ug = jax.random.uniform(ks[3], (2 * INTER,), jnp.float32, 0.5, 1.5)
        Wscale_dp = jax.random.uniform(ks[4], (HIDDEN,), jnp.float32, 0.5, 1.5)
        W_up = jax.random.normal(ks[5], (INTER, HIDDEN), dtype=jnp.float32) * 0.02
        W_gate = jax.random.normal(ks[6], (INTER, HIDDEN), dtype=jnp.float32) * 0.02
        W_down = jax.random.normal(ks[7], (HIDDEN, INTER), dtype=jnp.float32) * 0.02
        return {'input': inp, 'SU_ug': SU_ug, 'SU_dp': SU_dp, 'Wscale_ug': Wscale_ug, 'Wscale_dp': Wscale_dp, 'W_up': W_up, 'W_gate': W_gate, 'W_down': W_down}
    _L0_ffn_in = _L0_ffn_setup()
    _d = {'L0_attn_resid_pre': _L0_attn_in['resid_pre'], 'L0_attn_Wq': _L0_attn_in['Wq'], 'L0_attn_Wk': _L0_attn_in['Wk'], 'L0_attn_Wv': _L0_attn_in['Wv'], 'L0_attn_Wo': _L0_attn_in['Wo'], 'L0_ffn_SU_ug': _L0_ffn_in['SU_ug'], 'L0_ffn_SU_dp': _L0_ffn_in['SU_dp'], 'L0_ffn_Wscale_ug': _L0_ffn_in['Wscale_ug'], 'L0_ffn_Wscale_dp': _L0_ffn_in['Wscale_dp'], 'L0_ffn_W_up': _L0_ffn_in['W_up'], 'L0_ffn_W_gate': _L0_ffn_in['W_gate'], 'L0_ffn_W_down': _L0_ffn_in['W_down']}
    _x0 = _d['L0_attn_resid_pre']
    _d['L0_attn_resid_pre'] = jax.random.normal(jax.random.fold_in(jax.random.key(seed), 1), (2, 1024, 256), dtype=_x0.dtype)
    del _x0
    return _d

def reference(L0_attn_resid_pre, L0_attn_Wq, L0_attn_Wk, L0_attn_Wv, L0_attn_Wo, L0_ffn_SU_ug, L0_ffn_SU_dp, L0_ffn_Wscale_ug, L0_ffn_Wscale_dp, L0_ffn_W_up, L0_ffn_W_gate, L0_ffn_W_down):

    def _L0_attn_ref(resid_pre, Wq, Wk, Wv, Wo):
        import math
        import jax, jax.numpy as jnp
        import numpy as np
        B, S, D, H, DH = (2, 256, 256, 16, 128)

        def _alibi_slopes(n):

            def pow2(m):
                start = 2 ** (-2 ** (-(math.log2(m) - 3)))
                return [start * start ** i for i in range(m)]
            if math.log2(n).is_integer():
                return pow2(n)
            c = 2 ** math.floor(math.log2(n))
            return pow2(c) + _alibi_slopes(2 * c)[0::2][:n - c]

        def _alibi_mask(n_heads, q_len, kv_len):
            slopes = jnp.asarray(np.array(_alibi_slopes(n_heads), dtype=np.float32))
            bias = slopes[:, None, None] * jnp.arange(kv_len, dtype=jnp.float32)[None, None, :]
            i = jnp.arange(q_len)[:, None]
            j = jnp.arange(kv_len)[None, :]
            causal = jnp.where(j > i, -jnp.inf, 0.0).astype(jnp.float32)
            return causal[None, :, :] + bias
        b, s, d = resid_pre.shape
        q = (resid_pre @ Wq.T).reshape(b, s, H, DH)
        k = (resid_pre @ Wk.T).reshape(b, s, H, DH)
        v = (resid_pre @ Wv.T).reshape(b, s, H, DH)
        scores = jnp.einsum('bqhd,bkhd->bhqk', q, k) / math.sqrt(DH)
        scores = jnp.clip(scores, -1024.0, 1024.0)
        scores = scores + _alibi_mask(H, s, s)[None]
        attn = jax.nn.softmax(scores.astype(jnp.float32), axis=-1).astype(q.dtype)
        z = jnp.einsum('bhqk,bkhd->bqhd', attn, v)
        out = jnp.einsum('bqhd,ohd->bqo', z, Wo.reshape(d, H, DH))
        return out

    def _L0_ffn_ref(input, SU_ug, SU_dp, Wscale_ug, Wscale_dp, W_up, W_gate, W_down):
        import jax, jax.numpy as jnp
        import numpy as np
        HIDDEN = 256
        INTER = 1024
        SCALE = 64.0

        def fwht(x):
            orig_shape = x.shape
            n = orig_shape[-1]
            x = x.reshape(-1, n)
            h = 1
            while h < n:
                x = x.reshape(-1, n // (2 * h), 2, h)
                a, b = (x[:, :, 0, :], x[:, :, 1, :])
                x = jnp.stack([a + b, a - b], axis=2).reshape(-1, n)
                h *= 2
            return (x / jnp.sqrt(jnp.asarray(n, x.dtype))).reshape(orig_shape)
        n = SU_ug.shape[0]
        x = input.reshape(-1, n)
        x = fwht(x * SU_ug) / SCALE
        x_up = x @ W_up.T * (Wscale_ug[:INTER] * SCALE)
        x_gate = x @ W_gate.T * (Wscale_ug[INTER:] * SCALE)
        x = jax.nn.silu(x_gate) * x_up
        x = fwht(x * SU_dp) / SCALE
        x = x @ W_down.T * (Wscale_dp * SCALE)
        return x.reshape(input.shape)
    x = L0_attn_resid_pre
    x = x + 0.5 * _L0_ffn_ref(_layernorm(x, axis=-1), L0_ffn_SU_ug, L0_ffn_SU_dp, L0_ffn_Wscale_ug, L0_ffn_Wscale_dp, L0_ffn_W_up, L0_ffn_W_gate, L0_ffn_W_down)
    x = x + _L0_attn_ref(_layernorm(x, axis=-1), L0_attn_Wq, L0_attn_Wk, L0_attn_Wv, L0_attn_Wo)
    x = x + 0.5 * _L0_ffn_ref(_layernorm(x, axis=-1), L0_ffn_SU_ug, L0_ffn_SU_dp, L0_ffn_Wscale_ug, L0_ffn_Wscale_dp, L0_ffn_W_up, L0_ffn_W_gate, L0_ffn_W_down)
    return x

_drawn_inputs = setup_inputs


def setup_inputs(seed=0):
    import zlib

    import numpy as np

    out = dict(_drawn_inputs(seed))
    spreads = {}
    factors = {'L0_ffn_Wscale_ug': 4.977, 'L0_ffn_Wscale_dp': 6.887}
    for name, (base, spread) in spreads.items():
        noise = np.random.default_rng([zlib.crc32(name.encode()), seed]).standard_normal(out[name].shape)
        drawn = base * np.exp(spread * noise) if base else spread * noise
        out[name] = jnp.asarray(drawn.astype(out[name].dtype))
    for name, factor in factors.items():
        out[name] = (out[name] * factor).astype(out[name].dtype)
    return out
```

```python
from contextlib import ExitStack

import numpy as np
import concourse.bass as bass
from concourse import mybir

F32 = mybir.dt.float32
F32R = mybir.dt.float32r
ALU = mybir.AluOpType
ACT = mybir.ActivationFunctionType

P = 128
B, S, D = 2, 1024, 256
H, DH = 16, 128
INTER = 1024
T = B * S
DC = D // P
JC = INTER // P
GT = 512
G = T // GT
TT = GT // P
QT = S // P
HP = H // 2
HI, LO = 0, 1
EPS = 1e-5
FFN_SCALE = 64.0
CLIP = 1024.0
MASKED = -1e30


def mm3(nc, out, lhs, rhs, start, stop, **kw):
    nc.tensor.matmul(out, lhs[HI], rhs[HI], start=start, stop=False, **kw)
    nc.tensor.matmul(out, lhs[HI], rhs[LO], start=False, stop=False, **kw)
    return nc.tensor.matmul(out, lhs[LO], rhs[HI], start=False, stop=stop, **kw)


class LayerNorm:

    def __init__(self, nc, ctx, name):
        sb = lambda n, shape: ctx.enter_context(nc.sbuf_tensor(f"{name}_{n}", shape, F32))
        sem = lambda n: ctx.enter_context(nc.semaphore(f"{name}_{n}"))
        self.nc = nc
        self.stats, self.mean_var = sb("stats", [P, TT, 6]), sb("mean_var", [P, TT, 2])
        self.var, self.rstd, self.y = sb("var", [P, TT]), sb("rstd", [P, TT]), sb("y", [P, TT, D])
        self.stats_done, self.aggr_done = sem("stats_done"), sem("aggr_done")
        self.var_done, self.rstd_done, self.y_done = sem("var_done"), sem("rstd_done"), sem("y_done")
        self.turned, self.hi_done, self.lo_done = sem("turned"), sem("hi_done"), sem("lo_done")

    def dve_normalise(self, e, k, src, tables_in, tables):
        nc = self.nc
        for t in range(TT):
            last = nc.vector.bn_stats(self.stats[:, t, :], src[:, t, :])
        last.then_inc(self.stats_done, 1)
        e.wait_ge(tables_in, tables)
        e.wait_ge(self.stats_done, k + 1)
        for t in range(TT):
            last = nc.vector.bn_aggr(self.mean_var[:, t, :], self.stats[:, t, :])
        last.then_inc(self.aggr_done, 1)
        e.wait_ge(self.aggr_done, k + 1)
        nc.vector.tensor_scalar(self.var[:, :], self.mean_var[:, :, 1], EPS, None, ALU.add)\
            .then_inc(self.var_done, 1)
        e.wait_ge(self.rstd_done, k + 1)
        e.wait_ge(self.turned, DC * k)
        for t in range(TT):
            last = nc.vector.tensor_scalar(self.y[:, t, :], src[:, t, :], self.mean_var[:, t, 0:1],
                                           self.rstd[:, t:t + 1], ALU.subtract, ALU.mult)
        last.then_inc(self.y_done, 1)

    def pool_rstd(self, e, k, minus_half):
        e.wait_ge(self.var_done, k + 1)
        self.nc.gpsimd.tensor_tensor(self.rstd[:, :], self.var[:, :], minus_half, ALU.pow)\
            .then_inc(self.rstd_done, 1)

    def pe_turn(self, e, k, banks, ident):
        e.wait_ge(self.y_done, k + 1)
        for c in range(DC):
            for t in range(TT):
                last = self.nc.tensor.transpose(banks[c][:, t * P:(t + 1) * P],
                                                self.y[:, t, c * P:(c + 1) * P], ident)
            last.then_inc(self.turned, 1)

    def act_hi(self, e, k, banks, hi):
        for c in range(DC):
            e.wait_ge(self.turned, DC * k + c + 1)
            self.nc.scalar.activation(hi(c), banks[c][:, :], ACT.Copy).then_inc(self.hi_done, 1)

    def dve_lo(self, e, k, banks, hi, lo):
        for c in range(DC):
            e.wait_ge(self.hi_done, DC * k + c + 1)
            self.nc.vector.tensor_tensor(lo(c), banks[c][:, :], hi(c).bitcast(F32), ALU.subtract)\
                .then_inc(self.lo_done, 1)


def build(nc, x, wq, wk, wv, wo, su_ug, su_dp, ws_ug, ws_dp, w_up, w_gate, w_down,
          c_ident, c_had, c_bias, out):
    x2_d = nc.dram_tensor("x2_scratch", [T, D], F32).ap()
    z_d = nc.dram_tensor("z_scratch", [HP, 2, DH, T], F32).ap()
    wug_d = nc.dram_tensor("wug_scratch", [P, 2 * DC * 2 * INTER], F32).ap()
    wdn_d = nc.dram_tensor("wdn_scratch", [P, 2 * JC * D], F32).ap()
    wo_d = nc.dram_tensor("wo_scratch", [P, 2 * H * D], F32).ap()
    group_view = "(g t p) d -> g p t d"
    x_g = x.rearrange("b s d -> (b s) d").rearrange(group_view, g=G, p=P)
    x2_g = x2_d.rearrange(group_view, g=G, p=P)
    out_g = out.rearrange("b s d -> (b s) d").rearrange(group_view, g=G, p=P)

    whole = ExitStack()
    with whole:
        psum = [whole.enter_context(nc.psum_tensor(f"bank{i}", [P, 1024], F32)) for i in range(4)]
        bank = [psum[i // 2][:, i % 2 * 512:i % 2 * 512 + 512] for i in range(8)]
        ident = whole.enter_context(nc.sbuf_tensor("ident", [P, P], F32))
        minus_half = whole.enter_context(nc.sbuf_tensor("minus_half", [P, TT], F32))
        bias = whole.enter_context(nc.sbuf_tensor("bias", [P, 2, S], F32))
        shared = whole.enter_context(nc.sbuf_tensor("wo_or_tokens", [P, 2, DC * T], F32R))
        wo_t = shared[:, :, :].rearrange("p a (h o) -> p a h o", h=H)
        tok_t = shared[:, :, :].rearrange("p a (c t) -> p a c t", c=DC)
        tables_in = whole.enter_context(nc.semaphore("tables_in"))
        halves_set = whole.enter_context(nc.semaphore("halves_set"))
        wo_spilled = whole.enter_context(nc.semaphore("wo_spilled"))
        wo_back = whole.enter_context(nc.semaphore("wo_back"))
        TABLES = 16 * 3

        with ExitStack() as ctx:
            w_ug = ctx.enter_context(nc.sbuf_tensor("w_ug", [P, 2, DC, 2 * INTER], F32R))
            w_dn = ctx.enter_context(nc.sbuf_tensor("w_dn", [P, 2, JC, D], F32R))
            with ExitStack() as scratch:
                prepare(nc, scratch, bank, w_up, w_gate, w_down, wo, su_ug, su_dp, ws_ug, ws_dp,
                        c_ident, c_had, c_bias, ident, bias, minus_half, w_ug, w_dn, wo_t,
                        tables_in, halves_set)
            with ExitStack() as work:
                ffn(nc, work, 1, bank, x_g, x2_g, w_ug, w_dn, ident, minus_half, tables_in, TABLES,
                    halves_set, tok_t=tok_t, wo_spilled=wo_spilled,
                    spills=[(wo_d, shared[:, :, :].rearrange("p a n -> p (a n)")),
                            (wug_d, w_ug[:, :, :, :].rearrange("p a c n -> p (a c n)")),
                            (wdn_d, w_dn[:, :, :, :].rearrange("p a c n -> p (a c n)"))])
        with ExitStack() as work:
            attention(nc, work, psum, bank, wq, wk, wv, z_d, tok_t, bias, ident, tables_in, TABLES,
                      wo_d, shared, wo_back)
        with ExitStack() as ctx:
            w_ug = ctx.enter_context(nc.sbuf_tensor("w_ug_back", [P, 2, DC, 2 * INTER], F32R))
            w_dn = ctx.enter_context(nc.sbuf_tensor("w_dn_back", [P, 2, JC, D], F32R))
            ffn(nc, ctx, 2, bank, x2_g, out_g, w_ug, w_dn, ident, minus_half, tables_in, TABLES,
                halves_set, wo_t=wo_t, z_d=z_d, wo_back=wo_back,
                loads=[(wug_d, w_ug[:, :, :, :].rearrange("p a c n -> p (a c n)")),
                       (wdn_d, w_dn[:, :, :, :].rearrange("p a c n -> p (a c n)"))])


def prepare(nc, ctx, bank, w_up, w_gate, w_down, wo, su_ug, su_dp, ws_ug, ws_dp,
            c_ident, c_had, c_bias, ident, bias, minus_half, w_ug, w_dn, wo_t, tables_in, halves_set):
    sb = lambda n, shape, dt=F32: ctx.enter_context(nc.sbuf_tensor(n, shape, dt))
    sem = lambda n: ctx.enter_context(nc.semaphore(n))
    had_f = sb("had_f", [P, 2, P])
    had = sb("had", [P, 2, P], F32R)
    VECS = [(ws_ug, 2 * JC), (ws_dp, DC), (su_ug, DC), (su_dp, JC)]
    NV = sum(rows for _, rows in VECS)
    vec_rows, vec = sb("vec_rows", [NV, P]), sb("vec", [P, NV])
    row_ug, row_dn = vec[:, 0:2 * JC], vec[:, 2 * JC:2 * JC + DC]
    sign_ug, sign_dp = vec[:, 2 * JC + DC:2 * JC + 2 * DC], vec[:, 2 * JC + 2 * DC:NV]
    raw_ug = sb("raw_ug", [P, 2 * JC, D])
    raw_dn, raw_wo = sb("raw_dn", [P, DC, INTER]), sb("raw_wo", [P, DC, H * DH])
    ugT = sb("ugT", [P, 2, DC, 2 * INTER], F32R)
    dnT = sb("dnT", [P, 2, JC, D], F32R)
    vec_in, dn_in, wo_in = sem("vec_in"), sem("dn_in"), sem("wo_in")
    ug_in = [sem(f"ug_in{n}") for n in range(4)]
    had_done, vec_turned, vec_done = sem("had_done"), sem("vec_turned"), sem("vec_done")
    rows_done, ps_done, hi_done, lo_done = sem("rows_done"), sem("ps_done"), sem("hi_done"), sem("lo_done")

    JG = 4
    units = []

    def add(kind, *ab):
        units.append((kind, *ab))
    for g in range(JG):
        for c in range(DC):
            add("turn_ug", g, c)
        if g >= 1:
            for c in range(DC):
                add("had_ug", g - 1, c)
    for n in range(JC // 2):
        add("turn_dn", n, 0)
    for c in range(DC):
        add("had_ug", JG - 1, c)
    for n in range(H // 2):
        add("turn_wo", n, 0)
        add("had_dn", n, 0)
    order = {u: n for n, u in enumerate(units)}

    def parts(u):
        kind, a, b = u
        if kind == "turn_ug":
            return 512, [ugT[:, w, b, a * 512:(a + 1) * 512] for w in (HI, LO)], None
        if kind == "had_ug":
            return 512, [w_ug[:, w, b, a * 512:(a + 1) * 512] for w in (HI, LO)], sign_ug[:, b:b + 1]
        if kind == "turn_dn":
            return 512, [dnT[:, w, 2 * a:2 * a + 2, :].rearrange("p c o -> p (c o)") for w in (HI, LO)], None
        if kind == "turn_wo":
            return 512, [wo_t[:, w, 2 * a:2 * a + 2, :].rearrange("p c o -> p (c o)") for w in (HI, LO)], None
        return D, [w_dn[:, w, a, :] for w in (HI, LO)], sign_dp[:, a:a + 1]

    block = ctx.enter_context(nc.Block())

    @block.sync
    def _(sp):
        up_v = w_up.rearrange("(c p) d -> p c d", p=P)
        gate_v = w_gate.rearrange("(c p) d -> p c d", p=P)
        sp.dma_start(ident[:, :], c_ident).then_inc(tables_in, 16)
        sp.dma_start(raw_ug[:, 0:4, :], up_v[:, 0:4, :]).then_inc(ug_in[0], 16)
        sp.dma_start(raw_ug[:, 4:8, :], up_v[:, 4:8, :]).then_inc(ug_in[1], 16)
        sp.dma_start(raw_ug[:, 8:12, :], gate_v[:, 0:4, :]).then_inc(ug_in[2], 16)
        sp.dma_start(raw_ug[:, 12:16, :], gate_v[:, 4:8, :]).then_inc(ug_in[3], 16)
        sp.dma_start(raw_wo[:, :, :], wo.rearrange("(c p) n -> p c n", p=P)).then_inc(wo_in, 16)
        sp.wait_ge(tables_in, 16)
        sp.dma_start(bias[:, :, :], c_bias).then_inc(tables_in, 16)

    @block.gpsimd
    def _(pool):
        nc.gpsimd.memset(minus_half[:, :], -0.5).then_inc(halves_set, 1)
        pool.wait_ge(vec_done, 3)
        for n in range(2 * JC):
            if n % 4 == 0:
                pool.wait_ge(ug_in[n // 4], 16)
            nc.gpsimd.tensor_scalar(raw_ug[:, n, :], raw_ug[:, n, :], row_ug[:, n:n + 1], 1.0,
                                    ALU.mult, ALU.mult).then_inc(rows_done, 1)
        pool.wait_ge(dn_in, 16)
        for n in range(DC):
            nc.gpsimd.tensor_scalar(raw_dn[:, n, :], raw_dn[:, n, :], row_dn[:, n:n + 1], 1.0,
                                    ALU.mult, ALU.mult).then_inc(rows_done, 1)

    @block.tensor
    def _(pe):
        pe.wait_ge(tables_in, 16)
        pe.wait_ge(vec_in, 64)
        nc.tensor.transpose(bank[7][:, 0:NV], vec_rows[:, :], ident[0:NV, 0:NV]).then_inc(vec_turned, 1)
        for n, (kind, a, b) in enumerate(units):
            ps = bank[n % 8]
            if n == 7:
                pe.wait_ge(vec_done, 3)
            if n >= 8:
                pe.wait_ge(lo_done, n - 7)
            if kind == "turn_ug":
                pe.wait_ge(rows_done, 4 * (a + 1))
                for t in range(4):
                    last = nc.tensor.transpose(ps[:, t * P:(t + 1) * P],
                                               raw_ug[:, 4 * a + t, b * P:(b + 1) * P], ident[:, :])
            elif kind == "turn_dn":
                pe.wait_ge(rows_done, 2 * JC + DC)
                for i in range(2):
                    for c in range(DC):
                        last = nc.tensor.transpose(ps[:, (2 * i + c) * P:(2 * i + c + 1) * P],
                                                   raw_dn[:, c, (2 * a + i) * P:(2 * a + i + 1) * P],
                                                   ident[:, :])
            elif kind == "turn_wo":
                pe.wait_ge(wo_in, 16)
                for i in range(2):
                    for c in range(DC):
                        last = nc.tensor.transpose(ps[:, (2 * i + c) * P:(2 * i + c + 1) * P],
                                                   raw_wo[:, c, (2 * a + i) * P:(2 * a + i + 1) * P],
                                                   ident[:, :])
            elif kind == "had_ug":
                pe.wait_ge(had_done, 1)
                pe.wait_ge(lo_done, order["turn_ug", a, DC - 1] + 1)
                for c in range(DC):
                    for w in (HI, LO):
                        last = nc.tensor.matmul(ps, had[:, b * c % 2, :],
                                                ugT[:, w, c, a * 512:(a + 1) * 512],
                                                start=(c == 0 and w == HI), stop=(c == DC - 1 and w == LO))
            else:
                pe.wait_ge(lo_done, order["turn_dn", JC // 2 - 1, 0] + 1)
                for c in range(JC):
                    for w in (HI, LO):
                        last = nc.tensor.matmul(ps[:, 0:D], had[:, bin(a & c).count("1") % 2, :],
                                                dnT[:, w, c, :],
                                                start=(c == 0 and w == HI), stop=(c == JC - 1 and w == LO))
            last.then_inc(ps_done, 1)

    @block.scalar
    def _(act):
        row = 0
        for source, rows in VECS:
            act.dma_start(vec_rows[row:row + rows, :], source.rearrange("(c p) -> c p", p=P))\
                .then_inc(vec_in, 16)
            row += rows
        act.dma_start(raw_dn[:, :, :], w_down.rearrange("(c p) n -> p c n", p=P)).then_inc(dn_in, 16)
        act.wait_ge(tables_in, 16)
        act.dma_start(had_f[:, :, :], c_had).then_inc(tables_in, 16)
        act.wait_ge(vec_done, 3)
        for n, u in enumerate(units):
            cols, place, sign = parts(u)
            act.wait_ge(ps_done, n + 1)
            nc.scalar.activation(place[HI], bank[n % 8][:, 0:cols], ACT.Copy,
                                 scale=1.0 if sign is None else sign).then_inc(hi_done, 1)

    @block.vector
    def _(dve):
        dve.wait_ge(vec_turned, 1)
        turned, ug, dp = bank[7], 2 * JC + DC, 2 * JC + 2 * DC
        nc.vector.tensor_copy(vec[:, 0:ug], turned[:, 0:ug]).then_inc(vec_done, 1)
        nc.vector.tensor_scalar(sign_ug, turned[:, ug:dp], D ** -0.5 / FFN_SCALE * FFN_SCALE, None,
                                ALU.mult).then_inc(vec_done, 1)
        nc.vector.tensor_scalar(sign_dp, turned[:, dp:NV],
                                0.5 * INTER ** -0.5 / FFN_SCALE * FFN_SCALE, None,
                                ALU.mult).then_inc(vec_done, 1)
        dve.wait_ge(tables_in, 48)
        nc.vector.tensor_copy(had[:, :, :], had_f[:, :, :]).then_inc(had_done, 1)
        dve.wait_ge(vec_done, 3)
        for n, u in enumerate(units):
            cols, place, sign = parts(u)
            dve.wait_ge(hi_done, n + 1)
            hi = place[HI].bitcast(F32)
            if sign is None:
                last = nc.vector.tensor_tensor(place[LO], bank[n % 8][:, 0:cols], hi, ALU.subtract)
            else:
                last = nc.vector.scalar_tensor_tensor(place[LO], bank[n % 8][:, 0:cols], sign, hi,
                                                      ALU.mult, ALU.subtract)
            last.then_inc(lo_done, 1)


def ffn(nc, ctx, phase, bank, src_g, dst_g, w_ug, w_dn, ident, minus_half, tables_in, TABLES,
        halves_set, tok_t=None, wo_spilled=None, spills=(), wo_t=None, z_d=None, wo_back=None, loads=()):
    sb = lambda n, shape, dt=F32: ctx.enter_context(nc.sbuf_tensor(f"f{phase}_{n}", shape, dt))
    sem = lambda n: ctx.enter_context(nc.semaphore(f"f{phase}_{n}"))
    first_phase = phase == 1
    r = sb("r", [P, TT, D])
    res = sb("res", [P, TT, D])
    yT = sb("yT", [P, 2, DC, GT], F32R)
    silu = sb("silu", [P, 2, GT])
    hid = sb("hid", [P, 2, GT])
    hidT = sb("hidT", [P, 4, 2, GT], F32R)
    dst = sb("dst", [P, TT, D])
    gate_ps, up_ps, down_ps, pre_ps = bank[0:2], bank[2:4], bank[4:6], bank[6:8]
    ln = LayerNorm(nc, ctx, f"f{phase}_ln")
    ln2 = LayerNorm(nc, ctx, "f1_ln2") if first_phase else None
    src_in, weights_in, spilled = sem("src_in"), sem("weights_in"), sem("spilled")
    gu_done, silu_done, hid_done = sem("gu_done"), sem("silu_done"), sem("hid_done")
    hi_done, lo_done, down_done = sem("hi_done"), sem("lo_done"), sem("down_done")
    dst_done, dst_out, res_done = sem("dst_done"), sem("dst_out"), sem("res_done")
    pool_taken = sem("pool_taken")
    if not first_phase:
        src = sb("src", [P, TT, D])
        z_raw = sb("z_raw", [P, 2, 4, GT])
        z_t = sb("z_t", [P, 8, 2, GT], F32R)
        z_in, zhi_done, zlo_done, oproj_done, r_done = (
            [sem("z_in0"), sem("z_in1")], sem("zhi_done"), sem("zlo_done"), sem("oproj_done"), sem("r_done"))
    HEADS = {0: range(0, 6), 1: range(6, 11), 2: range(11, 16)}

    block = ctx.enter_context(nc.Block())

    def run(e, engine_body):
        engine_body(0, False, True)
        with e.Fori(1, G - 1) as g:
            engine_body(g, first_phase, True)
        engine_body(G - 1, first_phase, False)

    @block.sync
    def _(sp):
        sp.dma_start((r if first_phase else src)[:, :, :], src_g[0]).then_inc(src_in, 16)

        def load_heads(g, c):
            for i in range(2):
                sp.dma_start(z_raw[:, c % 2, 2 * i:2 * i + 2, :],
                             z_d[2 * c + i, :, :, bass.ds(g * GT, GT)].rearrange("h p t -> p h t"))\
                    .then_inc(z_in[c % 2], 16)

        if not first_phase:
            load_heads(0, 0)
            load_heads(0, 1)
            for c in range(2, 4):
                sp.wait_ge(zlo_done, 4 * c - 4)
                load_heads(0, c)
            for d, s in loads:
                sp.dma_start(s.bitcast(F32), d).then_inc(weights_in, 16)
        for n, (d, s) in enumerate(spills):
            sp.dma_start(d, s.bitcast(F32)).then_inc(wo_spilled if n == 0 else spilled, 16)

        def body(g, post, nxt):
            if nxt and first_phase:
                sp.wait_ge(res_done, g + 1)
                sp.dma_start(r[:, :, :], src_g[g + 1]).then_inc(src_in, 16)
            if nxt and not first_phase:
                sp.wait_ge(r_done, g + 1)
                sp.dma_start(src[:, :, :], src_g[g + 1]).then_inc(src_in, 16)
                for c in range(4):
                    sp.wait_ge(zlo_done, H * g + 12 + 4 * c)
                    load_heads(g + 1, c)
        run(sp, body)
        sp.wait_ge(dst_out, 16 * G)
        if spills:
            sp.wait_ge(spilled, 16 * (len(spills) - 1))

    @block.gpsimd
    def _(pool):
        pool.wait_ge(halves_set, 1)
        ln.pool_rstd(pool, 0, minus_half[:, :])

        def body(g, post, nxt):
            pool.wait_ge(ln.y_done, g + 1)
            if not (isinstance(g, int) and g == 0):
                pool.wait_ge(dst_done, g)
            pool.sem_inc(pool_taken, 1)
            nc.gpsimd.tensor_copy(res[:, :, :], r[:, :, :]).then_inc(res_done, 1)
            if post:
                ln2.pool_rstd(pool, g - 1, minus_half[:, :])
            if nxt:
                ln.pool_rstd(pool, g + 1, minus_half[:, :])
        run(pool, body)
        if first_phase:
            ln2.pool_rstd(pool, G - 1, minus_half[:, :])

    @block.tensor
    def _(pe):
        def up_gate(g, j, n):
            if not isinstance(n, int) or n >= 2:
                pe.wait_ge(hid_done, n - 1)
            if j == 0:
                pe.wait_ge(ln.lo_done, DC * (g + 1))
            for out_ps, first_col in ((gate_ps, INTER), (up_ps, 0)):
                for c in range(DC):
                    cols = slice(first_col + j * P, first_col + (j + 1) * P)
                    last = mm3(nc, out_ps[j % 2], [w_ug[:, w, c, cols] for w in (HI, LO)],
                               [yT[:, w, c, :] for w in (HI, LO)], c == 0, c == DC - 1)
            last.then_inc(gu_done, 1)

        def down(g, j, n):
            pe.wait_ge(lo_done, n + 1)
            if j == 0 and not (isinstance(g, int) and g == 0):
                pe.wait_ge(dst_done, g)
            for t in range(TT):
                last = mm3(nc, down_ps[t // 2][:, t % 2 * D:(t % 2 + 1) * D],
                           [hidT[:, j % 4, w, t * P:(t + 1) * P] for w in (HI, LO)],
                           [w_dn[:, w, j, :] for w in (HI, LO)],
                           j == 0 and t % 2 == 0, j == JC - 1, skip_group_check=True)
            last.then_inc(down_done, 1)

        def oproj(g, heads):
            for h in heads:
                if h == 0:
                    pe.wait_ge(wo_back, 16)
                    if not (isinstance(g, int) and g == 0):
                        pe.wait_ge(ln.lo_done, DC * g)
                pe.wait_ge(zlo_done, H * g + h + 1)
                for t in range(TT):
                    last = mm3(nc, pre_ps[t // 2][:, t % 2 * D:(t % 2 + 1) * D],
                               [z_t[:, h % 8, w, t * P:(t + 1) * P] for w in (HI, LO)],
                               [wo_t[:, w, h, :] for w in (HI, LO)],
                               h == 0 and t % 2 == 0, h == H - 1, skip_group_check=True)
                last.then_inc(oproj_done, 1)

        if not first_phase:
            oproj(0, range(H))
        ln.pe_turn(pe, 0, pre_ps, ident[:, :])
        if loads:
            pe.wait_ge(weights_in, 16 * len(loads))
        up_gate(0, 0, 0)
        up_gate(0, 1, 1)

        def body(g, post, nxt):
            for j in range(JC - 2):
                down(g, j, JC * g + j)
                up_gate(g, j + 2, JC * g + j + 2)
                if nxt and not first_phase and j in HEADS:
                    oproj(g + 1, HEADS[j])
                if post and j == 1:
                    ln2.pe_turn(pe, g - 1, pre_ps, ident[:, :])
            if nxt:
                if post:
                    pe.wait_ge(ln2.lo_done, DC * g)
                ln.pe_turn(pe, g + 1, pre_ps, ident[:, :])
            down(g, 6, JC * g + 6)
            if nxt:
                up_gate(g + 1, 0, JC * g + 8)
            down(g, 7, JC * g + 7)
            if nxt:
                up_gate(g + 1, 1, JC * g + 9)
        run(pe, body)
        if first_phase:
            ln2.pe_turn(pe, G - 1, pre_ps, ident[:, :])

    yT_hi, yT_lo = (lambda c: yT[:, HI, c, :]), (lambda c: yT[:, LO, c, :])

    def tok(w, g):
        return lambda c: tok_t[:, w, c, bass.ds(g * GT, GT)]

    @block.scalar
    def _(act):
        def silu_of(j, n):
            act.wait_ge(gu_done, n + 1)
            nc.scalar.activation(silu[:, j % 2, :], gate_ps[j % 2], ACT.Silu).then_inc(silu_done, 1)

        def hid_hi(j, n):
            act.wait_ge(hid_done, n + 1)
            if not isinstance(n, int) or n >= 4:
                act.wait_ge(down_done, n - 3)
            nc.scalar.activation(hidT[:, j % 4, HI, :], hid[:, j % 2, :], ACT.Copy).then_inc(hi_done, 1)

        def z_hi(g, heads):
            for h in heads:
                act.wait_ge(z_in[h // 4 % 2], 32 * 2 * g + 32 * (h // 8 + 1))
                if not (isinstance(g, int) and g == 0 and h < 8):
                    act.wait_ge(oproj_done, H * g + h - 7)
                nc.scalar.activation(z_t[:, h % 8, HI, :], z_raw[:, h // 4 % 2, h % 4, :], ACT.Copy)\
                    .then_inc(zhi_done, 1)

        if not first_phase:
            z_hi(0, range(H))
        ln.act_hi(act, 0, pre_ps, yT_hi)
        for j in range(2):
            silu_of(j, j)
            hid_hi(j, j)

        def tok_hi(k):
            act.wait_ge(wo_spilled, 16)
            for c in range(DC):
                act.wait_ge(ln2.turned, DC * k + c + 1)
                nc.scalar.activation(tok(HI, k)(c), pre_ps[c], ACT.Copy).then_inc(ln2.hi_done, 1)

        def store(g):
            act.wait_ge(dst_done, g + 1)
            act.dma_start(dst_g[g], dst[:, :, :]).then_inc(dst_out, 16)

        def body(g, post, nxt):
            if not (isinstance(g, int) and g == 0):
                store(g - 1)
            for j in range(JC - 2):
                silu_of(j + 2, JC * g + j + 2)
                hid_hi(j + 2, JC * g + j + 2)
                if nxt and not first_phase and j in HEADS:
                    z_hi(g + 1, HEADS[j])
                if post and j == 2:
                    tok_hi(g - 1)
            if nxt:
                ln.act_hi(act, g + 1, pre_ps, yT_hi)
                for j in range(2):
                    silu_of(j, JC * g + 8 + j)
                    hid_hi(j, JC * g + 8 + j)
        run(act, body)
        store(G - 1)
        if first_phase:
            tok_hi(G - 1)

    @block.vector
    def _(dve):
        def hid_of(j, n):
            dve.wait_ge(silu_done, n + 1)
            nc.vector.tensor_tensor(hid[:, j % 2, :], up_ps[j % 2], silu[:, j % 2, :], ALU.mult)\
                .then_inc(hid_done, 1)

        def hid_lo(j, n):
            dve.wait_ge(hi_done, n + 1)
            nc.vector.tensor_tensor(hidT[:, j % 4, LO, :], hid[:, j % 2, :],
                                    hidT[:, j % 4, HI, :].bitcast(F32), ALU.subtract).then_inc(lo_done, 1)

        def z_lo(g, heads):
            for h in heads:
                dve.wait_ge(zhi_done, H * g + h + 1)
                nc.vector.tensor_tensor(z_t[:, h % 8, LO, :], z_raw[:, h // 4 % 2, h % 4, :],
                                        z_t[:, h % 8, HI, :].bitcast(F32), ALU.subtract)\
                    .then_inc(zlo_done, 1)

        def residual(g):
            dve.wait_ge(oproj_done, H * (g + 1))
            dve.wait_ge(src_in, 16 * (g + 1))
            if not (isinstance(g, int) and g == 0):
                dve.wait_ge(res_done, g)
            for t in range(0, TT, 2):
                last = nc.vector.tensor_tensor(r[:, t:t + 2, :].rearrange("p t d -> p (t d)"),
                                               pre_ps[t // 2],
                                               src[:, t:t + 2, :].rearrange("p t d -> p (t d)"), ALU.add)
            last.then_inc(r_done, 1)
            dve.wait_ge(r_done, g + 1)

        def normalise(g):
            if first_phase:
                dve.wait_ge(src_in, 16 * (g + 1))
            else:
                residual(g)
            ln.dve_normalise(dve, g, r, tables_in, TABLES)

        def finish(g):
            dve.wait_ge(down_done, JC * (g + 1))
            dve.wait_ge(res_done, g + 1)
            if not (isinstance(g, int) and g == 0):
                dve.wait_ge(dst_out, 16 * g)
            for t in range(0, TT, 2):
                last = nc.vector.tensor_tensor(dst[:, t:t + 2, :].rearrange("p t d -> p (t d)"),
                                               down_ps[t // 2],
                                               res[:, t:t + 2, :].rearrange("p t d -> p (t d)"), ALU.add)
            last.then_inc(dst_done, 1)

        if not first_phase:
            z_lo(0, range(H))
        normalise(0)
        ln.dve_lo(dve, 0, pre_ps, yT_hi, yT_lo)
        for j in range(2):
            hid_of(j, j)
            hid_lo(j, j)

        def body(g, post, nxt):
            for j in range(JC - 2):
                if post and j == 0:
                    dve.wait_ge(dst_done, g)
                    ln2.dve_normalise(dve, g - 1, dst, tables_in, TABLES)
                hid_of(j + 2, JC * g + j + 2)
                hid_lo(j + 2, JC * g + j + 2)
                if nxt and not first_phase and j in HEADS:
                    z_lo(g + 1, HEADS[j])
                if post and j == 2:
                    ln2.dve_lo(dve, g - 1, pre_ps, tok(HI, g - 1), tok(LO, g - 1))
                if nxt and j == 3:
                    normalise(g + 1)
            if nxt:
                ln.dve_lo(dve, g + 1, pre_ps, yT_hi, yT_lo)
                hid_of(0, JC * g + 8)
                hid_lo(0, JC * g + 8)
            finish(g)
            if nxt:
                hid_of(1, JC * g + 9)
                hid_lo(1, JC * g + 9)
        run(dve, body)
        if first_phase:
            dve.wait_ge(dst_done, G)
            ln2.dve_normalise(dve, G - 1, dst, tables_in, TABLES)
            ln2.dve_lo(dve, G - 1, pre_ps, tok(HI, G - 1), tok(LO, G - 1))


def attention(nc, ctx, psum, bank, wq, wk, wv, z_d, tok_t, bias, ident, tables_in, TABLES,
              wo_d, shared, wo_back):
    sb = lambda n, shape, dt=F32: ctx.enter_context(nc.sbuf_tensor(n, shape, dt))
    sem = lambda n: ctx.enter_context(nc.semaphore(n))
    ST = 2 * B
    NU = ST * QT
    QG = QT // 2
    w_raw = sb("w_raw", [P, 3, 2, D])
    w_t = sb("w_t", [P, 3, 2, DC, 2 * DH], F32R)
    q_t = sb("q_t", [P, 2, 2, S], F32R)
    k_t = sb("k_t", [P, 2, 2, S], F32R)
    v = sb("v", [P, B, 2, QT, 2 * DH], F32R)
    prob = sb("prob", [P, 4, S])
    p_t = [sb("p_t0", [P, 2, QG, GT], F32R),
           sb("p_t1", [P, 2, QT, GT], F32R)]
    z_sb = sb("z_sb", [P, 2, GT])
    minus_max, row_sum, inv_sum = sb("minus_max", [P, 4]), sb("row_sum", [P, 4]), sb("inv_sum", [P, 4])
    turn_ps, z_ps, item_ps = bank[4:6], bank[6], bank[7]
    w_in = sem("w_in")
    s_done, clip_done, b_done = sem("s_done"), sem("clip_done"), sem("biased_done")
    exp_done, inv_done, norm_done = sem("exp_done"), sem("inv_done"), sem("norm_done")
    t_done, thi_done, tlo_done = sem("turned_done"), sem("thi_done"), sem("tlo_done")
    pv_done, z_done, z_out = sem("pv_done"), sem("z_done"), [sem("z_out0"), sem("z_out1")]
    item_done, ihi_done, ilo_done = sem("item_done"), sem("ihi_done"), sem("ilo_done")
    halved = sem("bias_halved")
    pool_taken, dve_taken = sem("pool_taken"), sem("dve_taken")
    WQ, WK, WV = range(3)

    START = [("w", WV), ("w", WQ), ("w", WK), ("q", 0, 0), ("k", 0, 0), ("q", 0, 1), ("k", 0, 1)]
    START += [("v", 0, n) for n in range(QT // 2)]

    def items(nxt):
        found = []
        for s in range(ST):
            for n, kind in enumerate([("q", 0), ("k", 0), ("q", 1), ("k", 1)]):
                item = (kind[0], (s + 1) % ST, kind[1])
                if s < ST - 1:
                    found.append((QT * s + 1 + n, item))
                elif nxt:
                    found.append((QT * s + 2 + n, item))
            for n in range(2):
                if s < 2 or nxt:
                    found.append((QT * s + 6 + n, ("v", 1 if s < 2 else 0, 2 * (s % 2) + n)))
        if nxt:
            found += [(2 * QT, ("w", WV)), (3 * QT, ("w", WQ)), (3 * QT + 1, ("w", WK))]
        return sorted(found, key=lambda f: f[0])

    ITEMS = len(items(True))
    NS = len(START)

    def number(hp, item, nxt=True):
        at = [i for _, i in items(nxt)].index(item)
        return NS + ITEMS * hp + at + 1

    def width(i):
        return (i + 1) * P

    def at_s(i):
        return 256 if i == 4 else 0

    def turn_banks(i):
        return [range(0, min(i + 1, 4))] + ([range(4, i + 1)] if i >= 4 else [])

    TB = sum(len(turn_banks(i)) for i in range(QT))

    def turn_number(hp, s, i, n):
        return ST * TB * hp + TB * s + sum(len(turn_banks(x)) for x in range(i)) + n

    PIECES = [(QT, 0, range(0, 2)), (QT + 1, 0, range(2, 4)),
              (QT + 4, 1, range(0, 2)), (QT + 5, 1, range(2, 4)), (QT + 6, 1, range(4, 8))]

    def is_first(hp):
        return isinstance(hp, int) and hp == 0

    def of_unit(hp, u, lag):
        v = u - lag
        if v >= NU or v < 0 and is_first(hp):
            return None
        return (hp - 1 if v < 0 else hp), v % NU // QT, v % QT

    def unit(hp, s, i):
        return NU * hp + QT * s + i

    def pieces(hp, u):
        found = []
        for step, g, tiles in PIECES:
            if (u - step) % QT == 0:
                s = (u - step) // QT
                if s < 0:
                    if is_first(hp):
                        continue
                    a, s = hp - 1, s + ST
                else:
                    a = hp
                if s >= ST:
                    continue
                found.append((a, s, g, tiles, tiles[0] == 0, tiles[-1] == (QG if g == 0 else QT) - 1))
        return found

    TAIL = QT

    def run(e, step, before=None, after=None):
        def iteration(hp, nxt):
            for u in range(NU + (0 if nxt else TAIL)):
                step(hp, u, nxt)
        iteration(0, True)
        with e.Fori(1, HP - 1) as hp:
            iteration(hp, True)
        iteration(HP - 1, False)

    def ring(u):
        return u % 4

    def turn_slot(s, i, n):
        return turn_number(0, s, i, n) % 2

    def places(what, w):
        if what[0] == "w":
            return w_t[:, what[1], w, :, :].rearrange("p c n -> p (c n)")
        if what[0] in "qk":
            return (q_t if what[0] == "q" else k_t)[:, what[1] % 2, w, what[2] * GT:(what[2] + 1) * GT]
        return v[:, what[1], w, 2 * what[2]:2 * what[2] + 2, :].rearrange("p c n -> p (c n)")

    def scale_of(what):
        return DH ** -0.5 if what[0] == "q" else 1.0

    def turned_place(s, i, n, w):
        tiles = turn_banks(i)[n]
        q = i % QG * P
        return p_t[i // QG][:, w, tiles[0]:tiles[-1] + 1, q:q + P]

    def item_at(hp, u, nxt):
        at = items(nxt)
        return [(NS + ITEMS * hp + n, item) for n, (w, item) in enumerate(at) if w == u]

    block = ctx.enter_context(nc.Block())

    @block.sync
    def _(sp):
        w_v = [w.rearrange("(a h p) d -> a p h d", h=2, p=P) for w in (wq, wk, wv)]

        def load_w(hp):
            for m in range(3):
                sp.dma_start(w_raw[:, m, :, :], w_v[m][hp]).then_inc(w_in, 16)

        def store_z(hp, u):
            for a, s, g, _, _, last in pieces(hp, u):
                if last:
                    sp.wait_ge(z_done, 2 * ST * a + 2 * s + g + 1)
                    first_col = s // 2 * S + g * GT
                    sp.dma_start(z_d[a, s % 2, :, first_col:first_col + GT], z_sb[:, g, :])\
                        .then_inc(z_out[g], 16)
        load_w(0)

        def step(hp, u, nxt):
            if u == 0 and nxt:
                sp.wait_ge(item_done, NS if is_first(hp) else NS + ITEMS * hp)
                load_w(hp + 1)
            if not nxt and u == 3 * QT:
                sp.wait_ge(item_done, number(hp, ("k", ST - 1, 1), nxt))
                sp.dma_start(shared[:, :, :].rearrange("p a n -> p (a n)").bitcast(F32), wo_d)\
                    .then_inc(wo_back, 16)
            store_z(hp, u)
        run(sp, step)
        for g in range(2):
            sp.wait_ge(z_out[g], 16 * ST * HP)

    @block.gpsimd
    def _(pool):
        def step(hp, u, nxt):
            f = of_unit(hp, u, 1)
            if f:
                a, s, i = f
                n = unit(a, s, i)
                pool.wait_ge(inv_done, n + 1)
                pool.sem_inc(pool_taken, 1)
                p = prob[:, ring(u - 1), 0:width(i)]
                nc.gpsimd.tensor_scalar(p, p, inv_sum[:, ring(u - 1):ring(u - 1) + 1], 1.0,
                                        ALU.mult, ALU.mult).then_inc(norm_done, 1)
            if u == 3 and not is_first(hp):
                halve(1, unit(hp, 0, 0))
            if u == 3 * QT + 3 and nxt:
                halve(0, unit(hp, 3, 0))

        def halve(head, used):
            pool.wait_ge(b_done, used)
            pool.sem_inc(pool_taken, 1)
            nc.gpsimd.tensor_scalar(bias[:, head, :], bias[:, head, :], 0.5, 1.0, ALU.mult, ALU.mult)\
                .then_inc(halved, 1)
        run(pool, step)

    @block.tensor
    def _(pe):
        def item(n, what, ps):
            if what[0] == "w":
                m = what[1]
                for c in range(DC):
                    for h in range(2):
                        last = nc.tensor.transpose(ps[:, (2 * c + h) * P:(2 * c + h + 1) * P],
                                                   w_raw[:, m, h, c * P:(c + 1) * P], ident[:, :])
            elif what[0] in "qk":
                m = WQ if what[0] == "q" else WK
                b, h = what[1] // 2, what[1] % 2
                first = b * S + what[2] * GT
                for c in range(DC):
                    last = mm3(nc, ps, [w_t[:, m, w, c, h * DH:(h + 1) * DH] for w in (HI, LO)],
                               [tok_t[:, w, c, first:first + GT] for w in (HI, LO)], c == 0, c == DC - 1)
            else:
                for k in range(2):
                    first = what[1] * S + (2 * what[2] + k) * P
                    for c in range(DC):
                        last = mm3(nc, ps[:, k * 2 * DH:(k + 1) * 2 * DH],
                                   [tok_t[:, w, c, first:first + P] for w in (HI, LO)],
                                   [w_t[:, WV, w, c, :] for w in (HI, LO)], c == 0, c == DC - 1)
            last.then_inc(item_done, 1)

        def step(hp, u, nxt):
            f = of_unit(hp, u, 0)
            if f:
                a, s, i = f
                n = unit(a, s, i)
                if not (is_first(a) and u < 2):
                    pe.wait_ge(b_done, n - 1)
                if i in (0, QG):
                    half = 0 if i == 0 else 1
                    if s > 0:
                        pe.wait_ge(ilo_done, number(a, ("k", s, half), nxt))
                    elif is_first(a):
                        pe.wait_ge(ilo_done, NS)
                    else:
                        pe.wait_ge(ilo_done, number(a - 1, ("k", s, half)))
                ps, o = psum[u % 2], at_s(i)
                k = 0
                while k < width(i):
                    m = min(width(i) - k, 512 - (o + k) % 512)
                    last = mm3(nc, ps[:, o + k:o + k + m],
                               [q_t[:, s % 2, w, i * P:(i + 1) * P] for w in (HI, LO)],
                               [k_t[:, s % 2, w, k:k + m] for w in (HI, LO)], True, True)
                    k += m
                last.then_inc(s_done, 1)
            f = of_unit(hp, u, 3)
            if f:
                a, s, i = f
                pe.wait_ge(norm_done, unit(a, s, i) + 1)
                for n, tiles in enumerate(turn_banks(i)):
                    at = turn_number(a, s, i, n)
                    if not (is_first(a) and at < 2):
                        pe.wait_ge(tlo_done, at - 1)
                    for t in tiles:
                        last = nc.tensor.transpose(
                            turn_ps[turn_slot(s, i, n)][:, (t - tiles[0]) * P:(t - tiles[0] + 1) * P],
                            prob[:, ring(u - 3), t * P:(t + 1) * P], ident[:, :])
                    last.then_inc(t_done, 1)
            for a, s, g, tiles, first, final in pieces(hp, u):
                if first:
                    n = 2 * ST * a + 2 * s + g
                    if not (is_first(a) and n == 0):
                        pe.wait_ge(z_done, n)
                    i = QG * g + QG - 1
                    pe.wait_ge(tlo_done, turn_number(a, s, i, len(turn_banks(i)) - 1) + 1)
                for t in tiles:
                    if first and t == 0 and g == 0 and s % 2 == 0:
                        if is_first(a) and s == 0:
                            pe.wait_ge(ilo_done, NS)
                        elif s == 0:
                            pe.wait_ge(ilo_done, number(a - 1, ("v", 0, 3)))
                        else:
                            pe.wait_ge(ilo_done, number(a, ("v", 1, 3), nxt))
                    q = max(0, t - QG * g) * P
                    last = mm3(nc, z_ps[:, q:GT],
                               [v[:, s // 2, w, t, s % 2 * DH:(s % 2 + 1) * DH] for w in (HI, LO)],
                               [p_t[g][:, w, t, q:GT] for w in (HI, LO)],
                               t == 0, final and t == tiles[-1])
                if final:
                    last.then_inc(pv_done, 1)
            for n, what in item_at(hp, u, nxt):
                if what == ("w", WV):
                    pe.wait_ge(w_in, 16 * 3 * (hp + 2))
                pe.wait_ge(ilo_done, n)
                item(n, what, item_ps)

        pe.wait_ge(w_in, 16 * 3)
        for n, what in enumerate(START):
            if n >= 4:
                pe.wait_ge(ilo_done, n - 3)
            if what[0] in "qkv":
                pe.wait_ge(ilo_done, START.index(("w", {"q": WQ, "k": WK, "v": WV}[what[0]])) + 1)
            item(n, what, bank[4 + n % 4])
        pe.wait_ge(ilo_done, NS)
        run(pe, step)

    @block.scalar
    def _(act):
        def item_hi(n, what, ps):
            act.wait_ge(item_done, n + 1)
            nc.scalar.activation(places(what, HI), ps, ACT.Copy, scale=scale_of(what)).then_inc(ihi_done, 1)

        for n, what in enumerate(START):
            item_hi(n, what, bank[4 + n % 4])

        def step(hp, u, nxt):
            f = of_unit(hp, u, 1)
            if f:
                a, s, i = f
                n = unit(a, s, i)
                act.wait_ge(b_done, n + 1)
                m = ring(u - 1)
                p = prob[:, m, 0:width(i)]
                nc.scalar.activation(p, p, ACT.Exp, scale=-1.0, bias=minus_max[:, m:m + 1],
                                     accum_out=row_sum[:, m:m + 1]).then_inc(exp_done, 1)
            for a, s, g, _, _, final in pieces(hp, u - 1):
                if final:
                    n = 2 * ST * a + 2 * s + g
                    act.wait_ge(pv_done, n + 1)
                    if not (is_first(a) and n < 2):
                        act.wait_ge(z_out[g], 16 * (ST * a + s))
                    nc.scalar.activation(z_sb[:, g, :], z_ps, ACT.Copy).then_inc(z_done, 1)
            f = of_unit(hp, u, 3)
            if f:
                a, s, i = f
                if i % QG == 0 and not (is_first(a) and s == 0):
                    act.wait_ge(pv_done, 2 * ST * a + 2 * s + i // QG - 1)
                for n, tiles in enumerate(turn_banks(i)):
                    act.wait_ge(t_done, turn_number(a, s, i, n) + 1)
                    nc.scalar.activation(turned_place(s, i, n, HI),
                                         turn_ps[turn_slot(s, i, n)][:, 0:len(tiles) * P]
                                         .rearrange("p (t q) -> p t q", q=P), ACT.Copy)\
                        .then_inc(thi_done, 1)
            for n, what in item_at(hp, u, nxt):
                item_hi(n, what, item_ps)
        run(act, step)

    @block.vector
    def _(dve):
        def item_lo(n, what, ps):
            dve.wait_ge(ihi_done, n + 1)
            nc.vector.scalar_tensor_tensor(places(what, LO), ps, scale_of(what),
                                           places(what, HI).bitcast(F32), ALU.mult, ALU.subtract)\
                .then_inc(ilo_done, 1)

        for n, what in enumerate(START):
            item_lo(n, what, bank[4 + n % 4])

        def step(hp, u, nxt):
            g = of_unit(hp, u, 4)
            if g:
                ga, gs, gi = g
                for k, tiles in enumerate(turn_banks(gi)):
                    dve.wait_ge(thi_done, turn_number(ga, gs, gi, k) + 1)
                    nc.vector.tensor_tensor(turned_place(gs, gi, k, LO),
                                            turn_ps[turn_slot(gs, gi, k)][:, 0:len(tiles) * P]
                                            .rearrange("p (t q) -> p t q", q=P),
                                            turned_place(gs, gi, k, HI).bitcast(F32), ALU.subtract)\
                        .then_inc(tlo_done, 1)
            for k, what in item_at(hp, u - 1, nxt) if u >= 1 else item_before(hp):
                item_lo(k, what, item_ps)
            f = of_unit(hp, u, 0)
            if f:
                a, s, i = f
                n = unit(a, s, i)
                o = at_s(i)
                ps = psum[u % 2][:, o:o + width(i)]
                dve.wait_ge(s_done, n + 1)
                nc.vector.tensor_scalar(ps, ps, CLIP, -CLIP, ALU.min, ALU.max).then_inc(clip_done, 1)
            g = of_unit(hp, u, 1)
            if g:
                ga, gs, gi = g
                m = ring(u - 1)
                dve.wait_ge(exp_done, unit(ga, gs, gi) + 1)
                nc.vector.reciprocal(inv_sum[:, m:m + 1], row_sum[:, m:m + 1]).then_inc(inv_done, 1)
            if f:
                m = ring(u)
                dve.wait_ge(clip_done, n + 1)
                if u >= 4 or not is_first(a):
                    t = of_unit(hp, u, 4)
                    dve.wait_ge(t_done, turn_number(*t, len(turn_banks(t[2])) - 1) + 1)
                if i == 0 and s < 2 and not is_first(a):
                    dve.wait_ge(halved, 2 * a - 1 + s)
                dve.sem_inc(dve_taken, 1)
                nc.vector.tensor_tensor_reduce(out=prob[:, m, 0:width(i)], in0=ps,
                                               in1=bias[:, s % 2, S - width(i):S], scale=-1.0,
                                               scalar=3e38, op0=ALU.add, op1=ALU.min,
                                               accum_out=minus_max[:, m:m + 1]).then_inc(b_done, 1)

        def item_before(hp):
            return [] if is_first(hp) else item_at(hp - 1, NU - 1, True)
        run(dve, step)


def tables():
    had = np.array([[1.0]])
    while had.shape[0] < P:
        had = np.block([[had, had], [had, -had]])
    first = 2.0 ** (-(2.0 ** -(np.log2(H) - 3)))
    column = np.arange(S) - (S - P)
    rows = np.where(column[None, :] > np.arange(P)[:, None], MASKED, column[None, :].astype(np.float64))
    slopes = np.array([first, first * first]).astype(np.float32)
    bias = np.stack([rows * slopes[0], rows * slopes[1]], 1)
    return (np.eye(P, dtype=np.float32), np.stack([had, -had], 1).astype(np.float32),
            bias.astype(np.float32))


_INS = ["L0_attn_resid_pre", "L0_attn_Wq", "L0_attn_Wk", "L0_attn_Wv", "L0_attn_Wo", "L0_ffn_SU_ug",
        "L0_ffn_SU_dp", "L0_ffn_Wscale_ug", "L0_ffn_Wscale_dp", "L0_ffn_W_up", "L0_ffn_W_gate",
        "L0_ffn_W_down"]


def kernel(**inputs):
    import concourse.bacc as bacc
    from concourse.bass_utils import run_bass_kernel_spmd

    nc = bacc.Bacc("TRN2", target_bir_lowering=False, num_devices=1)
    arrays, args = {}, []
    named = [(n, np.ascontiguousarray(inputs[n])) for n in _INS]
    named += list(zip(["c_ident", "c_had", "c_bias"], tables()))
    for name, a in named:
        arrays[f"in_{name}"] = a
        args.append(nc.dram_tensor(f"in_{name}", a.shape, F32, kind="ExternalInput").ap())
    out = nc.dram_tensor("out", [B, S, D], F32, kind="ExternalOutput").ap()
    build(nc, *args, out)
    r = run_bass_kernel_spmd(nc, [arrays], core_ids=[0])
    return r.results[0]["out"]
```

```python
from contextlib import ExitStack

import numpy as np
import concourse.bass as bass
from concourse import mybir

F32 = mybir.dt.float32
F32R = mybir.dt.float32r
ALU = mybir.AluOpType
ACT = mybir.ActivationFunctionType

P = 128
B, S, D = 2, 1024, 256
H, DH = 16, 128
INTER = 1024
T = B * S
DC = D // P
JC = INTER // P
GT = 512
G = T // GT
TT = GT // P
QT = S // P
HP = H // 2
HI, LO = 0, 1
EPS = 1e-5
FFN_SCALE = 64.0
CLIP = 1024.0
MASKED = -1e30


def mm3(nc, out, lhs, rhs, start, stop, **kw):
    nc.tensor.matmul(out, lhs[HI], rhs[HI], start=start, stop=False, **kw)
    nc.tensor.matmul(out, lhs[HI], rhs[LO], start=False, stop=False, **kw)
    return nc.tensor.matmul(out, lhs[LO], rhs[HI], start=False, stop=stop, **kw)


class LayerNorm:

    def __init__(self, nc, ctx, name):
        sb = lambda n, shape: ctx.enter_context(nc.sbuf_tensor(f"{name}_{n}", shape, F32))
        sem = lambda n: ctx.enter_context(nc.semaphore(f"{name}_{n}"))
        self.nc = nc
        self.stats, self.mean_var = sb("stats", [P, TT, 6]), sb("mean_var", [P, TT, 2])
        self.var, self.rstd, self.y = sb("var", [P, TT]), sb("rstd", [P, TT]), sb("y", [P, TT, D])
        self.stats_done, self.aggr_done = sem("stats_done"), sem("aggr_done")
        self.var_done, self.rstd_done, self.y_done = sem("var_done"), sem("rstd_done"), sem("y_done")
        self.turned, self.hi_done, self.lo_done = sem("turned"), sem("hi_done"), sem("lo_done")

    def dve_normalise(self, e, k, src, tables_in, tables):
        nc = self.nc
        for t in range(TT):
            last = nc.vector.bn_stats(self.stats[:, t, :], src[:, t, :])
        last.then_inc(self.stats_done, 1)
        e.wait_ge(tables_in, tables)
        e.wait_ge(self.stats_done, k + 1)
        for t in range(TT):
            last = nc.vector.bn_aggr(self.mean_var[:, t, :], self.stats[:, t, :])
        last.then_inc(self.aggr_done, 1)
        e.wait_ge(self.aggr_done, k + 1)
        nc.vector.tensor_scalar(self.var[:, :], self.mean_var[:, :, 1], EPS, None, ALU.add)\
            .then_inc(self.var_done, 1)
        e.wait_ge(self.rstd_done, k + 1)
        e.wait_ge(self.turned, DC * k)
        for t in range(TT):
            last = nc.vector.tensor_scalar(self.y[:, t, :], src[:, t, :], self.mean_var[:, t, 0:1],
                                           self.rstd[:, t:t + 1], ALU.subtract, ALU.mult)
        last.then_inc(self.y_done, 1)

    def pool_rstd(self, e, k, minus_half):
        e.wait_ge(self.var_done, k + 1)
        self.nc.gpsimd.tensor_tensor(self.rstd[:, :], self.var[:, :], minus_half, ALU.pow)\
            .then_inc(self.rstd_done, 1)

    def pe_turn(self, e, k, banks, ident):
        e.wait_ge(self.y_done, k + 1)
        for c in range(DC):
            for t in range(TT):
                last = self.nc.tensor.transpose(banks[c][:, t * P:(t + 1) * P],
                                                self.y[:, t, c * P:(c + 1) * P], ident)
            last.then_inc(self.turned, 1)

    def act_hi(self, e, k, banks, hi, chunks=range(DC)):
        for c in chunks:
            e.wait_ge(self.turned, DC * k + c + 1)
            self.nc.scalar.activation(hi(c), banks[c][:, :], ACT.Copy).then_inc(self.hi_done, 1)

    def dve_lo(self, e, k, banks, hi, lo, chunks=range(DC)):
        for c in chunks:
            e.wait_ge(self.hi_done, DC * k + c + 1)
            self.nc.vector.tensor_tensor(lo(c), banks[c][:, :], hi(c).bitcast(F32), ALU.subtract)\
                .then_inc(self.lo_done, 1)


def build(nc, x, wq, wk, wv, wo, su_ug, su_dp, ws_ug, ws_dp, w_up, w_gate, w_down,
          c_ident, c_had, c_bias, out):
    x2_d = nc.dram_tensor("x2_scratch", [T, D], F32).ap()
    z_d = nc.dram_tensor("z_scratch", [HP, 2, DH, T], F32).ap()
    wug_d = nc.dram_tensor("wug_scratch", [P, 2 * DC * 2 * INTER], F32).ap()
    wdn_d = nc.dram_tensor("wdn_scratch", [P, 2 * JC * D], F32).ap()
    group_view = "(g t p) d -> g p t d"
    x_g = x.rearrange("b s d -> (b s) d").rearrange(group_view, g=G, p=P)
    x2_g = x2_d.rearrange(group_view, g=G, p=P)
    out_g = out.rearrange("b s d -> (b s) d").rearrange(group_view, g=G, p=P)

    whole = ExitStack()
    with whole:
        psum = [whole.enter_context(nc.psum_tensor(f"bank{i}", [P, 1024], F32)) for i in range(4)]
        bank = [psum[i // 2][:, i % 2 * 512:i % 2 * 512 + 512] for i in range(8)]
        ident = whole.enter_context(nc.sbuf_tensor("ident", [P, P], F32))
        minus_half = whole.enter_context(nc.sbuf_tensor("minus_half", [P, TT], F32))
        bias = whole.enter_context(nc.sbuf_tensor("bias", [P, 2, S], F32))
        shared = whole.enter_context(nc.sbuf_tensor("tokens_or_wo", [P, 2, DC * T], F32R))
        wo_t = shared[:, :, :].rearrange("p a (h o) -> p a h o", h=H)
        tok_t = shared[:, :, :].rearrange("p a (c t) -> p a c t", c=DC)
        w_raw = whole.enter_context(nc.sbuf_tensor("w_raw", [P, 3, 2, D], F32))
        w_or_z = whole.enter_context(nc.sbuf_tensor("weights_or_z", [P, 2 * 4 * GT], F32R))
        w_t = w_or_z[:, 0:3 * 2 * DC * 2 * DH].rearrange("p (m a c n) -> p m a c n", m=3, a=2, c=DC)
        z_raw = w_or_z[:, :].bitcast(F32).rearrange("p (a h t) -> p a h t", a=2, h=4)
        sem = lambda n: whole.enter_context(nc.semaphore(n))
        tables_in, halves_set, x_in, w_in = sem("tables_in"), sem("halves_set"), sem("x_in"), sem("w_in")
        z_in = [sem("z_in0"), sem("z_in1")]
        TABLES = 16 * 2

        w_v = [w.rearrange("(a h p) d -> a p h d", h=2, p=P) for w in (wq, wk, wv)]

        def load_w(sp, hp):
            for m in range(3):
                sp.dma_start(w_raw[:, m, :, :], w_v[m][hp]).then_inc(w_in, 16)

        def load_heads(sp, g, c):
            for i in range(2):
                sp.dma_start(z_raw[:, c % 2, 2 * i:2 * i + 2, :],
                             z_d[2 * c + i, :, :, bass.ds(g * GT, GT)].rearrange("h p t -> p h t"))\
                    .then_inc(z_in[c % 2], 16)

        with ExitStack() as ctx:
            w_ug = ctx.enter_context(nc.sbuf_tensor("w_ug", [P, 2, DC, 2 * INTER], F32R))
            w_dn = ctx.enter_context(nc.sbuf_tensor("w_dn", [P, 2, JC, D], F32R))
            r = ctx.enter_context(nc.sbuf_tensor("f1_r", [P, TT, D], F32))
            ln = LayerNorm(nc, ctx, "f1_ln")
            with ExitStack() as scratch:
                prepare(nc, scratch, bank, w_up, w_gate, w_down, su_ug, su_dp, ws_ug, ws_dp,
                        c_ident, c_had, c_bias, ident, bias, minus_half, w_ug, w_dn,
                        tables_in, TABLES, halves_set, x_g[0], x_in, r, ln)
            with ExitStack() as work:
                ffn(nc, work, 1, bank, x_g, x2_g, w_ug, w_dn, ident, minus_half, tables_in, TABLES,
                    r, x_in, ln, tok_t=tok_t, load_w=load_w,
                    spills=[(wug_d, w_ug[:, :, :, :].rearrange("p a c n -> p (a c n)")),
                            (wdn_d, w_dn[:, :, :, :].rearrange("p a c n -> p (a c n)"))])
        with ExitStack() as work:
            attention(nc, work, psum, bank, wo, z_d, tok_t, wo_t, w_raw, w_t, w_in, load_w, load_heads,
                      bias, ident)
        with ExitStack() as ctx:
            w_ug = ctx.enter_context(nc.sbuf_tensor("w_ug_back", [P, 2, DC, 2 * INTER], F32R))
            w_dn = ctx.enter_context(nc.sbuf_tensor("w_dn_back", [P, 2, JC, D], F32R))
            r = ctx.enter_context(nc.sbuf_tensor("f2_r", [P, TT, D], F32))
            ln = LayerNorm(nc, ctx, "f2_ln")
            x2_in = ctx.enter_context(nc.semaphore("x2_in"))
            ffn(nc, ctx, 2, bank, x2_g, out_g, w_ug, w_dn, ident, minus_half, tables_in, TABLES,
                r, x2_in, ln, wo_t=wo_t, z_raw=z_raw, z_in=z_in, load_heads=load_heads,
                loads=[(wug_d, w_ug[:, :, :, :].rearrange("p a c n -> p (a c n)")),
                       (wdn_d, w_dn[:, :, :, :].rearrange("p a c n -> p (a c n)"))])


def prepare(nc, ctx, bank, w_up, w_gate, w_down, su_ug, su_dp, ws_ug, ws_dp,
            c_ident, c_had, c_bias, ident, bias, minus_half, w_ug, w_dn,
            tables_in, TABLES, halves_set, x_group, x_in, r, ln):
    sb = lambda n, shape, dt=F32: ctx.enter_context(nc.sbuf_tensor(n, shape, dt))
    sem = lambda n: ctx.enter_context(nc.semaphore(n))
    had_f = sb("had_f", [P, 2, P])
    had = sb("had", [P, 2, P], F32R)
    VECS = [(ws_ug, 2 * JC), (ws_dp, DC), (su_ug, DC), (su_dp, JC)]
    NV = sum(rows for _, rows in VECS)
    vec_rows, vec = sb("vec_rows", [NV, P]), sb("vec", [P, NV])
    row_ug, row_dn = vec[:, 0:2 * JC], vec[:, 2 * JC:2 * JC + DC]
    sign_ug, sign_dp = vec[:, 2 * JC + DC:2 * JC + 2 * DC], vec[:, 2 * JC + 2 * DC:NV]
    raw_ug = sb("raw_ug", [P, 2 * JC, D])
    raw_dn = sb("raw_dn", [P, DC, INTER])
    ugT = sb("ugT", [P, 2, DC, 2 * INTER], F32R)
    dnT = sb("dnT", [P, 2, JC, D], F32R)
    vec_in, dn_in = sem("vec_in"), sem("dn_in")
    ug_in = [sem(f"ug_in{n}") for n in range(4)]
    had_in, had_done = sem("had_in"), sem("had_done")
    vec_turned, vec_done = sem("vec_turned"), sem("vec_done")
    rows_done, ps_done, hi_done, lo_done = sem("rows_done"), sem("ps_done"), sem("hi_done"), sem("lo_done")

    JG = 4
    units = []

    def add(kind, *ab):
        units.append((kind, *ab))
    for g in range(JG):
        for c in range(DC):
            add("turn_ug", g, c)
        if g >= 1:
            for c in range(DC):
                add("had_ug", g - 1, c)
    for n in range(JC // 2):
        add("turn_dn", n, 0)
    for c in range(DC):
        add("had_ug", JG - 1, c)
    for n in range(JC):
        add("had_dn", n, 0)
    order = {u: n for n, u in enumerate(units)}

    def parts(u):
        kind, a, b = u
        if kind == "turn_ug":
            return 512, [ugT[:, w, b, a * 512:(a + 1) * 512] for w in (HI, LO)], None
        if kind == "had_ug":
            return 512, [w_ug[:, w, b, a * 512:(a + 1) * 512] for w in (HI, LO)], sign_ug[:, b:b + 1]
        if kind == "turn_dn":
            return 512, [dnT[:, w, 2 * a:2 * a + 2, :].rearrange("p c o -> p (c o)") for w in (HI, LO)], None
        return D, [w_dn[:, w, a, :] for w in (HI, LO)], sign_dp[:, a:a + 1]

    block = ctx.enter_context(nc.Block())

    @block.sync
    def _(sp):
        up_v = w_up.rearrange("(c p) d -> p c d", p=P)
        gate_v = w_gate.rearrange("(c p) d -> p c d", p=P)
        sp.dma_start(ident[:, :], c_ident).then_inc(tables_in, 16)
        sp.dma_start(raw_ug[:, 0:4, :], up_v[:, 0:4, :]).then_inc(ug_in[0], 16)
        sp.dma_start(raw_ug[:, 4:8, :], up_v[:, 4:8, :]).then_inc(ug_in[1], 16)
        sp.dma_start(raw_ug[:, 8:12, :], gate_v[:, 0:4, :]).then_inc(ug_in[2], 16)
        sp.dma_start(raw_ug[:, 12:16, :], gate_v[:, 4:8, :]).then_inc(ug_in[3], 16)
        sp.dma_start(r[:, :, :], x_group).then_inc(x_in, 16)
        sp.wait_ge(tables_in, 16)
        sp.dma_start(bias[:, :, :], c_bias).then_inc(tables_in, 16)

    @block.gpsimd
    def _(pool):
        nc.gpsimd.memset(minus_half[:, :], -0.5).then_inc(halves_set, 1)
        pool.wait_ge(vec_done, 3)
        for n in range(2 * JC):
            if n % 4 == 0:
                pool.wait_ge(ug_in[n // 4], 16)
            nc.gpsimd.tensor_scalar(raw_ug[:, n, :], raw_ug[:, n, :], row_ug[:, n:n + 1], 1.0,
                                    ALU.mult, ALU.mult).then_inc(rows_done, 1)
        pool.wait_ge(dn_in, 16)
        for n in range(DC):
            nc.gpsimd.tensor_scalar(raw_dn[:, n, :], raw_dn[:, n, :], row_dn[:, n:n + 1], 1.0,
                                    ALU.mult, ALU.mult).then_inc(rows_done, 1)
        pool.wait_ge(halves_set, 1)
        ln.pool_rstd(pool, 0, minus_half[:, :])

    @block.tensor
    def _(pe):
        pe.wait_ge(tables_in, 16)
        pe.wait_ge(vec_in, 64)
        nc.tensor.transpose(bank[7][:, 0:NV], vec_rows[:, :], ident[0:NV, 0:NV]).then_inc(vec_turned, 1)
        for n, (kind, a, b) in enumerate(units):
            ps = bank[n % 8]
            if n == 7:
                pe.wait_ge(vec_done, 3)
            if n >= 8:
                pe.wait_ge(lo_done, n - 7)
            if kind == "turn_ug":
                pe.wait_ge(rows_done, 4 * (a + 1))
                for t in range(4):
                    last = nc.tensor.transpose(ps[:, t * P:(t + 1) * P],
                                               raw_ug[:, 4 * a + t, b * P:(b + 1) * P], ident[:, :])
            elif kind == "turn_dn":
                pe.wait_ge(rows_done, 2 * JC + DC)
                for i in range(2):
                    for c in range(DC):
                        last = nc.tensor.transpose(ps[:, (2 * i + c) * P:(2 * i + c + 1) * P],
                                                   raw_dn[:, c, (2 * a + i) * P:(2 * a + i + 1) * P],
                                                   ident[:, :])
            elif kind == "had_ug":
                pe.wait_ge(had_done, 1)
                pe.wait_ge(lo_done, order["turn_ug", a, DC - 1] + 1)
                for c in range(DC):
                    for w in (HI, LO):
                        last = nc.tensor.matmul(ps, had[:, b * c % 2, :],
                                                ugT[:, w, c, a * 512:(a + 1) * 512],
                                                start=(c == 0 and w == HI), stop=(c == DC - 1 and w == LO))
            else:
                pe.wait_ge(lo_done, order["turn_dn", JC // 2 - 1, 0] + 1)
                for c in range(JC):
                    for w in (HI, LO):
                        last = nc.tensor.matmul(ps[:, 0:D], had[:, bin(a & c).count("1") % 2, :],
                                                dnT[:, w, c, :],
                                                start=(c == 0 and w == HI), stop=(c == JC - 1 and w == LO))
            last.then_inc(ps_done, 1)

    @block.scalar
    def _(act):
        row = 0
        for source, rows in VECS:
            act.dma_start(vec_rows[row:row + rows, :], source.rearrange("(c p) -> c p", p=P))\
                .then_inc(vec_in, 16)
            row += rows
        act.dma_start(had_f[:, :, :], c_had).then_inc(had_in, 16)
        act.dma_start(raw_dn[:, :, :], w_down.rearrange("(c p) n -> p c n", p=P)).then_inc(dn_in, 16)
        act.wait_ge(vec_done, 3)
        for n, u in enumerate(units):
            cols, place, sign = parts(u)
            act.wait_ge(ps_done, n + 1)
            nc.scalar.activation(place[HI], bank[n % 8][:, 0:cols], ACT.Copy,
                                 scale=1.0 if sign is None else sign).then_inc(hi_done, 1)

    @block.vector
    def _(dve):
        dve.wait_ge(vec_turned, 1)
        turned, ug, dp = bank[7], 2 * JC + DC, 2 * JC + 2 * DC
        nc.vector.tensor_copy(vec[:, 0:ug], turned[:, 0:ug]).then_inc(vec_done, 1)
        nc.vector.tensor_scalar(sign_ug, turned[:, ug:dp], D ** -0.5 / FFN_SCALE * FFN_SCALE, None,
                                ALU.mult).then_inc(vec_done, 1)
        nc.vector.tensor_scalar(sign_dp, turned[:, dp:NV],
                                0.5 * INTER ** -0.5 / FFN_SCALE * FFN_SCALE, None,
                                ALU.mult).then_inc(vec_done, 1)
        dve.wait_ge(had_in, 16)
        nc.vector.tensor_copy(had[:, :, :], had_f[:, :, :]).then_inc(had_done, 1)
        dve.wait_ge(vec_done, 3)
        for n, u in enumerate(units):
            cols, place, sign = parts(u)
            dve.wait_ge(hi_done, n + 1)
            hi = place[HI].bitcast(F32)
            if sign is None:
                last = nc.vector.tensor_tensor(place[LO], bank[n % 8][:, 0:cols], hi, ALU.subtract)
            else:
                last = nc.vector.scalar_tensor_tensor(place[LO], bank[n % 8][:, 0:cols], sign, hi,
                                                      ALU.mult, ALU.subtract)
            last.then_inc(lo_done, 1)
            if u == ("turn_dn", 0, 0):
                dve.wait_ge(x_in, 16)
                ln.dve_normalise(dve, 0, r, tables_in, TABLES)


def ffn(nc, ctx, phase, bank, src_g, dst_g, w_ug, w_dn, ident, minus_half, tables_in, TABLES,
        r, src_in, ln, tok_t=None, load_w=None, spills=(), wo_t=None, z_raw=None, z_in=None,
        load_heads=None, loads=()):
    sb = lambda n, shape, dt=F32: ctx.enter_context(nc.sbuf_tensor(f"f{phase}_{n}", shape, dt))
    sem = lambda n: ctx.enter_context(nc.semaphore(f"f{phase}_{n}"))
    first_phase = phase == 1
    res = sb("res", [P, TT, D])
    yT = sb("yT", [P, 2, DC, GT], F32R)
    silu = sb("silu", [P, 2, GT])
    hid = sb("hid", [P, 2, GT])
    hidT = sb("hidT", [P, 4, 2, GT], F32R)
    dst = sb("dst", [P, TT, D])
    gate_ps, up_ps, down_ps, pre_ps = bank[0:2], bank[2:4], bank[4:6], bank[6:8]
    ln2 = LayerNorm(nc, ctx, "f1_ln2") if first_phase else None
    weights_in, spilled = sem("weights_in"), sem("spilled")
    gu_done, silu_done, hid_done = sem("gu_done"), sem("silu_done"), sem("hid_done")
    hi_done, lo_done, down_done = sem("hi_done"), sem("lo_done"), sem("down_done")
    dst_done, dst_out, res_done = sem("dst_done"), sem("dst_out"), sem("res_done")
    pool_taken = sem("pool_taken")
    if not first_phase:
        src = sb("src", [P, TT, D])
        z_t = sb("z_t", [P, 8, 2, GT], F32R)
        zhi_done, zlo_done, oproj_done, r_done = (
            sem("zhi_done"), sem("zlo_done"), sem("oproj_done"), sem("r_done"))
    HEADS = {0: range(0, 6), 1: range(6, 11), 2: range(11, 16)}

    block = ctx.enter_context(nc.Block())

    def run(e, engine_body):
        engine_body(0, False, True)
        with e.Fori(1, G - 1) as g:
            engine_body(g, first_phase, True)
        engine_body(G - 1, first_phase, False)

    @block.sync
    def _(sp):
        if not first_phase:
            sp.dma_start(src[:, :, :], src_g[0]).then_inc(src_in, 16)
            for c in range(2, 4):
                sp.wait_ge(zlo_done, 4 * c - 4)
                load_heads(sp, 0, c)
            for d, s in loads:
                sp.dma_start(s.bitcast(F32), d).then_inc(weights_in, 16)
        if first_phase:
            load_w(sp, 0)
        for d, s in spills:
            sp.dma_start(d, s.bitcast(F32)).then_inc(spilled, 16)

        def body(g, post, nxt):
            if nxt and first_phase:
                sp.wait_ge(res_done, g + 1)
                sp.dma_start(r[:, :, :], src_g[g + 1]).then_inc(src_in, 16)
            if nxt and not first_phase:
                sp.wait_ge(r_done, g + 1)
                sp.dma_start(src[:, :, :], src_g[g + 1]).then_inc(src_in, 16)
                for c in range(4):
                    sp.wait_ge(zlo_done, H * g + 12 + 4 * c)
                    load_heads(sp, g + 1, c)
        run(sp, body)
        sp.wait_ge(dst_out, 16 * G)
        if spills:
            sp.wait_ge(spilled, 16 * len(spills))

    @block.gpsimd
    def _(pool):
        if not first_phase:
            ln.pool_rstd(pool, 0, minus_half[:, :])

        def body(g, post, nxt):
            pool.wait_ge(ln.y_done, g + 1)
            if not (isinstance(g, int) and g == 0):
                pool.wait_ge(dst_done, g)
            pool.sem_inc(pool_taken, 1)
            nc.gpsimd.tensor_copy(res[:, :, :], r[:, :, :]).then_inc(res_done, 1)
            if post:
                ln2.pool_rstd(pool, g - 1, minus_half[:, :])
            if nxt:
                ln.pool_rstd(pool, g + 1, minus_half[:, :])
        run(pool, body)
        if first_phase:
            ln2.pool_rstd(pool, G - 1, minus_half[:, :])

    @block.tensor
    def _(pe):
        def up_gate(g, j, n):
            if not isinstance(n, int) or n >= 2:
                pe.wait_ge(hid_done, n - 1)
            if j == 0:
                pe.wait_ge(ln.lo_done, DC * (g + 1))
            for out_ps, first_col in ((gate_ps, INTER), (up_ps, 0)):
                for c in range(DC):
                    cols = slice(first_col + j * P, first_col + (j + 1) * P)
                    last = mm3(nc, out_ps[j % 2], [w_ug[:, w, c, cols] for w in (HI, LO)],
                               [yT[:, w, c, :] for w in (HI, LO)], c == 0, c == DC - 1)
            last.then_inc(gu_done, 1)

        def down(g, j, n):
            pe.wait_ge(lo_done, n + 1)
            if j == 0 and not (isinstance(g, int) and g == 0):
                pe.wait_ge(dst_done, g)
            for t in range(TT):
                last = mm3(nc, down_ps[t // 2][:, t % 2 * D:(t % 2 + 1) * D],
                           [hidT[:, j % 4, w, t * P:(t + 1) * P] for w in (HI, LO)],
                           [w_dn[:, w, j, :] for w in (HI, LO)],
                           j == 0 and t % 2 == 0, j == JC - 1, skip_group_check=True)
            last.then_inc(down_done, 1)

        def oproj(g, heads):
            for h in heads:
                if h == 0 and not (isinstance(g, int) and g == 0):
                    pe.wait_ge(ln.lo_done, DC * g)
                pe.wait_ge(zlo_done, H * g + h + 1)
                for t in range(TT):
                    last = mm3(nc, pre_ps[t // 2][:, t % 2 * D:(t % 2 + 1) * D],
                               [z_t[:, h % 8, w, t * P:(t + 1) * P] for w in (HI, LO)],
                               [wo_t[:, w, h, :] for w in (HI, LO)],
                               h == 0 and t % 2 == 0, h == H - 1, skip_group_check=True)
                last.then_inc(oproj_done, 1)

        if not first_phase:
            oproj(0, range(H))
        ln.pe_turn(pe, 0, pre_ps, ident[:, :])
        if loads:
            pe.wait_ge(weights_in, 16 * len(loads))
        up_gate(0, 0, 0)
        up_gate(0, 1, 1)

        def body(g, post, nxt):
            for j in range(JC - 2):
                down(g, j, JC * g + j)
                up_gate(g, j + 2, JC * g + j + 2)
                if nxt and not first_phase and j in HEADS:
                    oproj(g + 1, HEADS[j])
                if post and j == 1:
                    ln2.pe_turn(pe, g - 1, pre_ps, ident[:, :])
            if nxt:
                if post:
                    pe.wait_ge(ln2.lo_done, DC * g)
                ln.pe_turn(pe, g + 1, pre_ps, ident[:, :])
            for j in range(JC - 2, JC):
                down(g, j, JC * g + j)
            if nxt:
                for j in range(2):
                    up_gate(g + 1, j, JC * (g + 1) + j)
        run(pe, body)
        if first_phase:
            ln2.pe_turn(pe, G - 1, pre_ps, ident[:, :])

    yT_hi, yT_lo = (lambda c: yT[:, HI, c, :]), (lambda c: yT[:, LO, c, :])

    def tok(w, g):
        return lambda c: tok_t[:, w, c, bass.ds(g * GT, GT)]

    @block.scalar
    def _(act):
        def silu_of(j, n):
            act.wait_ge(gu_done, n + 1)
            nc.scalar.activation(silu[:, j % 2, :], gate_ps[j % 2], ACT.Silu).then_inc(silu_done, 1)

        def hid_hi(j, n):
            act.wait_ge(hid_done, n + 1)
            if not isinstance(n, int) or n >= 4:
                act.wait_ge(down_done, n - 3)
            nc.scalar.activation(hidT[:, j % 4, HI, :], hid[:, j % 2, :], ACT.Copy).then_inc(hi_done, 1)

        def z_hi(g, heads):
            for h in heads:
                act.wait_ge(z_in[h // 4 % 2], 32 * 2 * g + 32 * (h // 8 + 1))
                if not (isinstance(g, int) and g == 0 and h < 8):
                    act.wait_ge(oproj_done, H * g + h - 7)
                nc.scalar.activation(z_t[:, h % 8, HI, :], z_raw[:, h // 4 % 2, h % 4, :], ACT.Copy)\
                    .then_inc(zhi_done, 1)

        if not first_phase:
            z_hi(0, range(H))
        ln.act_hi(act, 0, pre_ps, yT_hi)
        for j in range(2):
            silu_of(j, j)
            hid_hi(j, j)

        def tok_hi(k):
            for c in range(DC):
                act.wait_ge(ln2.turned, DC * k + c + 1)
                nc.scalar.activation(tok(HI, k)(c), pre_ps[c], ACT.Copy).then_inc(ln2.hi_done, 1)

        def store(g):
            act.wait_ge(dst_done, g + 1)
            act.dma_start(dst_g[g], dst[:, :, :]).then_inc(dst_out, 16)

        def body(g, post, nxt):
            if not (isinstance(g, int) and g == 0):
                store(g - 1)
            for j in range(JC - 2):
                if nxt and not first_phase and j in HEADS:
                    z_hi(g + 1, HEADS[j])
                silu_of(j + 2, JC * g + j + 2)
                if nxt and j == JC - 3:
                    ln.act_hi(act, g + 1, pre_ps, yT_hi, [0])
                hid_hi(j + 2, JC * g + j + 2)
                if post and j == 2:
                    tok_hi(g - 1)
            if nxt:
                ln.act_hi(act, g + 1, pre_ps, yT_hi, [1])
                for j in range(2):
                    silu_of(j, JC * (g + 1) + j)
                    hid_hi(j, JC * (g + 1) + j)
        run(act, body)
        store(G - 1)
        if first_phase:
            tok_hi(G - 1)

    @block.vector
    def _(dve):
        def hid_of(j, n):
            dve.wait_ge(silu_done, n + 1)
            nc.vector.tensor_tensor(hid[:, j % 2, :], up_ps[j % 2], silu[:, j % 2, :], ALU.mult)\
                .then_inc(hid_done, 1)

        def hid_lo(j, n):
            dve.wait_ge(hi_done, n + 1)
            nc.vector.tensor_tensor(hidT[:, j % 4, LO, :], hid[:, j % 2, :],
                                    hidT[:, j % 4, HI, :].bitcast(F32), ALU.subtract).then_inc(lo_done, 1)

        def z_lo(g, heads):
            for h in heads:
                dve.wait_ge(zhi_done, H * g + h + 1)
                nc.vector.tensor_tensor(z_t[:, h % 8, LO, :], z_raw[:, h // 4 % 2, h % 4, :],
                                        z_t[:, h % 8, HI, :].bitcast(F32), ALU.subtract)\
                    .then_inc(zlo_done, 1)

        def residual(g):
            dve.wait_ge(oproj_done, H * (g + 1))
            dve.wait_ge(src_in, 16 * (g + 1))
            if not (isinstance(g, int) and g == 0):
                dve.wait_ge(res_done, g)
            for t in range(0, TT, 2):
                last = nc.vector.tensor_tensor(r[:, t:t + 2, :].rearrange("p t d -> p (t d)"),
                                               pre_ps[t // 2],
                                               src[:, t:t + 2, :].rearrange("p t d -> p (t d)"), ALU.add)
            last.then_inc(r_done, 1)
            dve.wait_ge(r_done, g + 1)

        def normalise(g):
            if first_phase:
                dve.wait_ge(src_in, 16 * (g + 1))
            else:
                residual(g)
            ln.dve_normalise(dve, g, r, tables_in, TABLES)

        def finish(g):
            dve.wait_ge(down_done, JC * (g + 1))
            dve.wait_ge(res_done, g + 1)
            if not (isinstance(g, int) and g == 0):
                dve.wait_ge(dst_out, 16 * g)
            for t in range(0, TT, 2):
                last = nc.vector.tensor_tensor(dst[:, t:t + 2, :].rearrange("p t d -> p (t d)"),
                                               down_ps[t // 2],
                                               res[:, t:t + 2, :].rearrange("p t d -> p (t d)"), ALU.add)
            last.then_inc(dst_done, 1)

        if not first_phase:
            z_lo(0, range(H))
            normalise(0)
        ln.dve_lo(dve, 0, pre_ps, yT_hi, yT_lo)
        for j in range(2):
            hid_of(j, j)
            hid_lo(j, j)

        def body(g, post, nxt):
            for j in range(JC - 2):
                if post and j == 0:
                    dve.wait_ge(dst_done, g)
                    ln2.dve_normalise(dve, g - 1, dst, tables_in, TABLES)
                if nxt and not first_phase and j in HEADS:
                    z_lo(g + 1, HEADS[j])
                hid_of(j + 2, JC * g + j + 2)
                if nxt and j == JC - 3:
                    ln.dve_lo(dve, g + 1, pre_ps, yT_hi, yT_lo, [0])
                hid_lo(j + 2, JC * g + j + 2)
                if post and j == 2:
                    ln2.dve_lo(dve, g - 1, pre_ps, tok(HI, g - 1), tok(LO, g - 1))
                if nxt and j == 3:
                    normalise(g + 1)
            if nxt:
                ln.dve_lo(dve, g + 1, pre_ps, yT_hi, yT_lo, [1])
            finish(g)
            if nxt:
                for j in range(2):
                    hid_of(j, JC * (g + 1) + j)
                    hid_lo(j, JC * (g + 1) + j)
        run(dve, body)
        if first_phase:
            dve.wait_ge(dst_done, G)
            ln2.dve_normalise(dve, G - 1, dst, tables_in, TABLES)
            ln2.dve_lo(dve, G - 1, pre_ps, tok(HI, G - 1), tok(LO, G - 1))


def attention(nc, ctx, psum, bank, wo, z_d, tok_t, wo_t, w_raw, w_t, w_in, load_w, load_heads,
              bias, ident):
    sb = lambda n, shape, dt=F32: ctx.enter_context(nc.sbuf_tensor(n, shape, dt))
    sem = lambda n: ctx.enter_context(nc.semaphore(n))
    ST = 2 * B
    NU = ST * QT
    QG = QT // 2
    q_t = sb("q_t", [P, 2, 2, S], F32R)
    k_t = sb("k_t", [P, 2, 2, S], F32R)
    v = sb("v", [P, B, 2, QT, 2 * DH], F32R)
    prob = sb("prob", [P, QT * (QT + 1) // 2 * P])
    p_t = [sb("p_t0", [P, 2, QG, GT], F32R),
           sb("p_t1", [P, 2, QT, GT], F32R)]
    z_sb = sb("z_sb", [P, 2, GT])
    minus_max, row_sum, inv_sum = sb("minus_max", [P, QT]), sb("row_sum", [P, QT]), sb("inv_sum", [P, QT])
    turn_ps, z_ps, item_ps = bank[4:6], bank[6], bank[7]
    wo_in = [sem(f"wo_in{n}") for n in range(3)]
    s_done, clip_done, b_done = sem("s_done"), sem("clip_done"), sem("biased_done")
    exp_done, inv_done, norm_done = sem("exp_done"), sem("inv_done"), sem("norm_done")
    t_done, thi_done, tlo_done = sem("turned_done"), sem("thi_done"), sem("tlo_done")
    pv_done, z_done, z_out = sem("pv_done"), sem("z_done"), [sem("z_out0"), sem("z_out1")]
    item_done, ihi_done, ilo_done = sem("item_done"), sem("ihi_done"), sem("ilo_done")
    halved = sem("bias_halved")
    pool_taken, dve_taken = sem("pool_taken"), sem("dve_taken")
    WQ, WK, WV = range(3)

    WO_STEP = 3 * QT
    START = [("w", WV), ("w", WQ), ("w", WK), ("q", 0, 0), ("k", 0, 0), ("q", 0, 1), ("k", 0, 1)]
    START += [("v", 0, n) for n in range(QT // 2)]

    def items(nxt):
        found = []
        for s in range(ST):
            for n, kind in enumerate([("q", 0), ("k", 0), ("q", 1), ("k", 1)]):
                item = (kind[0], (s + 1) % ST, kind[1])
                if s < ST - 1:
                    found.append((QT * s + 1 + n, item))
                elif nxt:
                    found.append((QT * s + 2 + n, item))
            for n in range(2):
                if s < 2 or nxt:
                    found.append((QT * s + 6 + n, ("v", 1 if s < 2 else 0, 2 * (s % 2) + n)))
        if not nxt:
            found += [(WO_STEP + n, ("o", n)) for n in range(H // 2)]
        if nxt:
            found += [(2 * QT, ("w", WV)), (3 * QT, ("w", WQ)), (3 * QT + 1, ("w", WK))]
        return sorted(found, key=lambda f: f[0])

    ITEMS = len(items(True))
    NS = len(START)

    def number(hp, item, nxt=True):
        at = [i for _, i in items(nxt)].index(item)
        return NS + ITEMS * hp + at + 1

    def width(i):
        return (i + 1) * P

    def at_s(i):
        return 256 if i == 4 else 0

    def turn_banks(i):
        return [range(0, min(i + 1, 4))] + ([range(4, i + 1)] if i >= 4 else [])

    TB = sum(len(turn_banks(i)) for i in range(QT))

    def turn_number(hp, s, i, n):
        return ST * TB * hp + TB * s + sum(len(turn_banks(x)) for x in range(i)) + n

    LAG = 5
    PIECES = [(QG + LAG + 1, 0, range(0, 2)), (QG + LAG + 2, 0, range(2, 4)), (QT + LAG + 1, 1, range(0, 2)),
              (QT + LAG + 2, 1, range(2, 4)), (QT + LAG + 3, 1, range(4, 8))]

    def is_first(hp):
        return isinstance(hp, int) and hp == 0

    def of_unit(hp, u, lag):
        v = u - lag
        if v >= NU or v < 0 and is_first(hp):
            return None
        return (hp - 1 if v < 0 else hp), v % NU // QT, v % QT

    def unit(hp, s, i):
        return NU * hp + QT * s + i

    def pieces(hp, u):
        found = []
        for step, g, tiles in PIECES:
            if (u - step) % QT == 0:
                s = (u - step) // QT
                if s < 0:
                    if is_first(hp):
                        continue
                    a, s = hp - 1, s + ST
                else:
                    a = hp
                if s >= ST:
                    continue
                found.append((a, s, g, tiles, tiles[0] == 0, tiles[-1] == (QG if g == 0 else QT) - 1))
        return found

    TAIL = LAG + 5

    def run(e, step, before=None, after=None):
        def iteration(hp, nxt):
            for u in range(NU + (0 if nxt else TAIL)):
                step(hp, u, nxt)
        iteration(0, True)
        with e.Fori(1, HP - 1) as hp:
            iteration(hp, True)
        iteration(HP - 1, False)

    def prob_of(i):
        return prob[:, i * (i + 1) // 2 * P:(i + 1) * (i + 2) // 2 * P]

    def turn_slot(s, i, n):
        return turn_number(0, s, i, n) % 2

    def places(what, w):
        if what[0] == "w":
            return w_t[:, what[1], w, :, :].rearrange("p c n -> p (c n)")
        if what[0] == "o":
            return wo_t[:, w, 2 * what[1]:2 * what[1] + 2, :].rearrange("p h o -> p (h o)")
        if what[0] in "qk":
            return (q_t if what[0] == "q" else k_t)[:, what[1] % 2, w, what[2] * GT:(what[2] + 1) * GT]
        return v[:, what[1], w, 2 * what[2]:2 * what[2] + 2, :].rearrange("p c n -> p (c n)")

    def scale_of(what):
        return DH ** -0.5 if what[0] == "q" else 1.0

    def turned_place(s, i, n, w):
        tiles = turn_banks(i)[n]
        q = i % QG * P
        return p_t[i // QG][:, w, tiles[0]:tiles[-1] + 1, q:q + P]

    def item_at(hp, u, nxt):
        at = items(nxt)
        return [(NS + ITEMS * hp + n, item) for n, (w, item) in enumerate(at) if w == u]

    block = ctx.enter_context(nc.Block())

    @block.sync
    def _(sp):
        wo_v = wo.rearrange("(c p) n -> p c n", p=P)

        def store_z(hp, u):
            for a, s, g, _, _, last in pieces(hp, u):
                if last:
                    sp.wait_ge(z_done, 2 * ST * a + 2 * s + g + 1)
                    first_col = s // 2 * S + g * GT
                    sp.dma_start(z_d[a, s % 2, :, first_col:first_col + GT], z_sb[:, g, :])\
                        .then_inc(z_out[g], 16)
        def step(hp, u, nxt):
            if u == 0 and nxt:
                sp.wait_ge(item_done, NS if is_first(hp) else NS + ITEMS * hp)
                load_w(sp, hp + 1)
            if not nxt:
                for n in range(H // 2):
                    if u == (0 if n < 3 else WO_STEP + n - 2):
                        sp.wait_ge(item_done, NS + ITEMS * hp if n < 3 else number(hp, ("o", n - 3), nxt))
                        sp.dma_start(w_raw[:, n % 3, :, :], wo_v[:, :, n * 2 * DH:(n + 1) * 2 * DH])\
                            .then_inc(wo_in[n % 3], 16)
                if u == 3 * QT:
                    sp.wait_ge(ilo_done, number(hp, ("k", ST - 1, 1), nxt))
                    for g in range(2):
                        sp.wait_ge(z_out[g], 16 * ST * 4)
                    load_heads(sp, 0, 0)
                    load_heads(sp, 0, 1)
            store_z(hp, u)
        run(sp, step)
        for g in range(2):
            sp.wait_ge(z_out[g], 16 * ST * HP)

    @block.gpsimd
    def _(pool):
        def step(hp, u, nxt):
            f = of_unit(hp, u, 1)
            if f:
                a, s, i = f
                n = unit(a, s, i)
                pool.wait_ge(inv_done, n + 1)
                pool.sem_inc(pool_taken, 1)
                nc.gpsimd.tensor_scalar(prob_of(i), prob_of(i), inv_sum[:, i:i + 1], 1.0,
                                        ALU.mult, ALU.mult).then_inc(norm_done, 1)
            if u == 3 and not is_first(hp):
                halve(1, unit(hp, 0, 0))
            if u == 3 * QT + 3 and nxt:
                halve(0, unit(hp, 3, 0))

        def halve(head, used):
            pool.wait_ge(b_done, used)
            pool.sem_inc(pool_taken, 1)
            nc.gpsimd.tensor_scalar(bias[:, head, :], bias[:, head, :], 0.5, 1.0, ALU.mult, ALU.mult)\
                .then_inc(halved, 1)
        run(pool, step)

    @block.tensor
    def _(pe):
        def item(n, what, ps):
            if what[0] == "w":
                m = what[1]
                for c in range(DC):
                    for h in range(2):
                        last = nc.tensor.transpose(ps[:, (2 * c + h) * P:(2 * c + h + 1) * P],
                                                   w_raw[:, m, h, c * P:(c + 1) * P], ident[:, :])
            elif what[0] == "o":
                for i in range(2):
                    for c in range(DC):
                        last = nc.tensor.transpose(ps[:, (2 * i + c) * P:(2 * i + c + 1) * P],
                                                   w_raw[:, what[1] % 3, c, i * P:(i + 1) * P], ident[:, :])
            elif what[0] in "qk":
                m = WQ if what[0] == "q" else WK
                b, h = what[1] // 2, what[1] % 2
                first = b * S + what[2] * GT
                for c in range(DC):
                    last = mm3(nc, ps, [w_t[:, m, w, c, h * DH:(h + 1) * DH] for w in (HI, LO)],
                               [tok_t[:, w, c, first:first + GT] for w in (HI, LO)], c == 0, c == DC - 1)
            else:
                for k in range(2):
                    first = what[1] * S + (2 * what[2] + k) * P
                    for c in range(DC):
                        last = mm3(nc, ps[:, k * 2 * DH:(k + 1) * 2 * DH],
                                   [tok_t[:, w, c, first:first + P] for w in (HI, LO)],
                                   [w_t[:, WV, w, c, :] for w in (HI, LO)], c == 0, c == DC - 1)
            last.then_inc(item_done, 1)

        def step(hp, u, nxt):
            f = of_unit(hp, u, 0)
            if f:
                a, s, i = f
                n = unit(a, s, i)
                if not (is_first(a) and u < 2):
                    pe.wait_ge(b_done, n - 1)
                if i in (0, QG):
                    half = 0 if i == 0 else 1
                    if s > 0:
                        pe.wait_ge(ilo_done, number(a, ("k", s, half), nxt))
                    elif is_first(a):
                        pe.wait_ge(ilo_done, NS)
                    else:
                        pe.wait_ge(ilo_done, number(a - 1, ("k", s, half)))
                ps, o = psum[u % 2], at_s(i)
                k = 0
                while k < width(i):
                    m = min(width(i) - k, 512 - (o + k) % 512)
                    last = mm3(nc, ps[:, o + k:o + k + m],
                               [q_t[:, s % 2, w, i * P:(i + 1) * P] for w in (HI, LO)],
                               [k_t[:, s % 2, w, k:k + m] for w in (HI, LO)], True, True)
                    k += m
                last.then_inc(s_done, 1)
            f = of_unit(hp, u, LAG)
            if f:
                a, s, i = f
                pe.wait_ge(norm_done, unit(a, s, i) + 1)
                for n, tiles in enumerate(turn_banks(i)):
                    at = turn_number(a, s, i, n)
                    if not (is_first(a) and at < 2):
                        pe.wait_ge(tlo_done, at - 1)
                    for t in tiles:
                        last = nc.tensor.transpose(
                            turn_ps[turn_slot(s, i, n)][:, (t - tiles[0]) * P:(t - tiles[0] + 1) * P],
                            prob_of(i)[:, t * P:(t + 1) * P], ident[:, :])
                    last.then_inc(t_done, 1)
            for a, s, g, tiles, first, final in pieces(hp, u):
                if first:
                    n = 2 * ST * a + 2 * s + g
                    if not (is_first(a) and n == 0):
                        pe.wait_ge(z_done, n)
                    i = QG * g + QG - 1
                    pe.wait_ge(tlo_done, turn_number(a, s, i, len(turn_banks(i)) - 1) + 1)
                for t in tiles:
                    if first and t == 0 and g == 0 and s % 2 == 0:
                        if is_first(a) and s == 0:
                            pe.wait_ge(ilo_done, NS)
                        elif s == 0:
                            pe.wait_ge(ilo_done, number(a - 1, ("v", 0, 3)))
                        else:
                            pe.wait_ge(ilo_done, number(a, ("v", 1, 3), nxt))
                    q = max(0, t - QG * g) * P
                    last = mm3(nc, z_ps[:, q:GT],
                               [v[:, s // 2, w, t, s % 2 * DH:(s % 2 + 1) * DH] for w in (HI, LO)],
                               [p_t[g][:, w, t, q:GT] for w in (HI, LO)],
                               t == 0, final and t == tiles[-1])
                if final:
                    last.then_inc(pv_done, 1)
            for n, what in item_at(hp, u, nxt):
                if what == ("w", WV):
                    pe.wait_ge(w_in, 16 * 3 * (hp + 2))
                if what[0] == "o":
                    pe.wait_ge(wo_in[what[1] % 3], 16 * (what[1] // 3 + 1))
                pe.wait_ge(ilo_done, n)
                item(n, what, item_ps)

        for n, what in enumerate(START):
            if n >= 4:
                pe.wait_ge(ilo_done, n - 3)
            if what[0] in "qkv":
                pe.wait_ge(ilo_done, START.index(("w", {"q": WQ, "k": WK, "v": WV}[what[0]])) + 1)
            item(n, what, bank[4 + n % 4])
        pe.wait_ge(ilo_done, NS)
        run(pe, step)

    @block.scalar
    def _(act):
        def item_hi(n, what, ps):
            act.wait_ge(item_done, n + 1)
            nc.scalar.activation(places(what, HI), ps, ACT.Copy, scale=scale_of(what)).then_inc(ihi_done, 1)

        for n, what in enumerate(START):
            item_hi(n, what, bank[4 + n % 4])

        def step(hp, u, nxt):
            f = of_unit(hp, u, 1)
            if f:
                a, s, i = f
                n = unit(a, s, i)
                act.wait_ge(b_done, n + 1)
                nc.scalar.activation(prob_of(i), prob_of(i), ACT.Exp, scale=-1.0,
                                     bias=minus_max[:, i:i + 1], accum_out=row_sum[:, i:i + 1])\
                    .then_inc(exp_done, 1)
            for a, s, g, _, _, final in pieces(hp, u - 1):
                if final:
                    n = 2 * ST * a + 2 * s + g
                    act.wait_ge(pv_done, n + 1)
                    if not (is_first(a) and n < 2):
                        act.wait_ge(z_out[g], 16 * (ST * a + s))
                    nc.scalar.activation(z_sb[:, g, :], z_ps, ACT.Copy).then_inc(z_done, 1)
            f = of_unit(hp, u, LAG)
            if f:
                a, s, i = f
                if i % QG == 0 and not (is_first(a) and s == 0):
                    act.wait_ge(pv_done, 2 * ST * a + 2 * s + i // QG - 1)
                for n, tiles in enumerate(turn_banks(i)):
                    act.wait_ge(t_done, turn_number(a, s, i, n) + 1)
                    nc.scalar.activation(turned_place(s, i, n, HI),
                                         turn_ps[turn_slot(s, i, n)][:, 0:len(tiles) * P]
                                         .rearrange("p (t q) -> p t q", q=P), ACT.Copy)\
                        .then_inc(thi_done, 1)
            for n, what in item_at(hp, u, nxt):
                item_hi(n, what, item_ps)
        run(act, step)

    @block.vector
    def _(dve):
        def item_lo(n, what, ps):
            dve.wait_ge(ihi_done, n + 1)
            nc.vector.scalar_tensor_tensor(places(what, LO), ps, scale_of(what),
                                           places(what, HI).bitcast(F32), ALU.mult, ALU.subtract)\
                .then_inc(ilo_done, 1)

        for n, what in enumerate(START):
            item_lo(n, what, bank[4 + n % 4])

        def step(hp, u, nxt):
            g = of_unit(hp, u, LAG + 1)
            if g:
                ga, gs, gi = g
                for k, tiles in enumerate(turn_banks(gi)):
                    dve.wait_ge(thi_done, turn_number(ga, gs, gi, k) + 1)
                    nc.vector.tensor_tensor(turned_place(gs, gi, k, LO),
                                            turn_ps[turn_slot(gs, gi, k)][:, 0:len(tiles) * P]
                                            .rearrange("p (t q) -> p t q", q=P),
                                            turned_place(gs, gi, k, HI).bitcast(F32), ALU.subtract)\
                        .then_inc(tlo_done, 1)
            for k, what in item_at(hp, u - 1, nxt) if u >= 1 else item_before(hp):
                item_lo(k, what, item_ps)
            f = of_unit(hp, u, 0)
            if f:
                a, s, i = f
                n = unit(a, s, i)
                o = at_s(i)
                ps = psum[u % 2][:, o:o + width(i)]
                dve.wait_ge(s_done, n + 1)
                nc.vector.tensor_scalar(ps, ps, CLIP, -CLIP, ALU.min, ALU.max).then_inc(clip_done, 1)
            g = of_unit(hp, u, 1)
            if g:
                ga, gs, gi = g
                dve.wait_ge(exp_done, unit(ga, gs, gi) + 1)
                nc.vector.reciprocal(inv_sum[:, gi:gi + 1], row_sum[:, gi:gi + 1]).then_inc(inv_done, 1)
            if f:
                dve.wait_ge(clip_done, n + 1)
                if u >= QT or not is_first(a):
                    t = of_unit(hp, u, QT)
                    dve.wait_ge(t_done, turn_number(*t, len(turn_banks(t[2])) - 1) + 1)
                if i == 0 and s < 2 and not is_first(a):
                    dve.wait_ge(halved, 2 * a - 1 + s)
                dve.sem_inc(dve_taken, 1)
                nc.vector.tensor_tensor_reduce(out=prob_of(i), in0=ps,
                                               in1=bias[:, s % 2, S - width(i):S], scale=-1.0,
                                               scalar=3e38, op0=ALU.add, op1=ALU.min,
                                               accum_out=minus_max[:, i:i + 1]).then_inc(b_done, 1)

        def item_before(hp):
            return [] if is_first(hp) else item_at(hp - 1, NU - 1, True)
        run(dve, step)


def tables():
    had = np.array([[1.0]])
    while had.shape[0] < P:
        had = np.block([[had, had], [had, -had]])
    first = 2.0 ** (-(2.0 ** -(np.log2(H) - 3)))
    column = np.arange(S) - (S - P)
    rows = np.where(column[None, :] > np.arange(P)[:, None], MASKED, column[None, :].astype(np.float64))
    slopes = np.array([first, first * first]).astype(np.float32)
    bias = np.stack([rows * slopes[0], rows * slopes[1]], 1)
    return (np.eye(P, dtype=np.float32), np.stack([had, -had], 1).astype(np.float32),
            bias.astype(np.float32))


_INS = ["L0_attn_resid_pre", "L0_attn_Wq", "L0_attn_Wk", "L0_attn_Wv", "L0_attn_Wo", "L0_ffn_SU_ug",
        "L0_ffn_SU_dp", "L0_ffn_Wscale_ug", "L0_ffn_Wscale_dp", "L0_ffn_W_up", "L0_ffn_W_gate",
        "L0_ffn_W_down"]


def kernel(**inputs):
    import concourse.bacc as bacc
    from concourse.bass_utils import run_bass_kernel_spmd

    nc = bacc.Bacc("TRN2", target_bir_lowering=False, num_devices=1)
    arrays, args = {}, []
    named = [(n, np.ascontiguousarray(inputs[n])) for n in _INS]
    named += list(zip(["c_ident", "c_had", "c_bias"], tables()))
    for name, a in named:
        arrays[f"in_{name}"] = a
        args.append(nc.dram_tensor(f"in_{name}", a.shape, F32, kind="ExternalInput").ap())
    out = nc.dram_tensor("out", [B, S, D], F32, kind="ExternalOutput").ap()
    build(nc, *args, out)
    r = run_bass_kernel_spmd(nc, [arrays], core_ids=[0])
    return r.results[0]["out"]
```

```python
from contextlib import ExitStack

import numpy as np
import concourse.bass as bass
from concourse import mybir

F32 = mybir.dt.float32
F32R = mybir.dt.float32r
ALU = mybir.AluOpType
ACT = mybir.ActivationFunctionType

P = 128
B, S, D = 2, 1024, 256
H, DH = 16, 128
INTER = 1024
T = B * S
DC = D // P
JC = INTER // P
GT = 512
G = T // GT
TT = GT // P
QT = S // P
HP = H // 2
HI, LO = 0, 1
EPS = 1e-5
FFN_SCALE = 64.0
CLIP = 1024.0
MASKED = -1e30


def mm3(nc, out, lhs, rhs, start, stop, **kw):
    nc.tensor.matmul(out, lhs[HI], rhs[HI], start=start, stop=False, **kw)
    nc.tensor.matmul(out, lhs[HI], rhs[LO], start=False, stop=False, **kw)
    return nc.tensor.matmul(out, lhs[LO], rhs[HI], start=False, stop=stop, **kw)


class LayerNorm:

    def __init__(self, nc, ctx, name):
        sb = lambda n, shape: ctx.enter_context(nc.sbuf_tensor(f"{name}_{n}", shape, F32))
        sem = lambda n: ctx.enter_context(nc.semaphore(f"{name}_{n}"))
        self.nc = nc
        self.stats, self.mean_var = sb("stats", [P, TT, 6]), sb("mean_var", [P, TT, 2])
        self.var, self.rstd, self.y = sb("var", [P, TT]), sb("rstd", [P, TT]), sb("y", [P, TT, D])
        self.stats_done, self.aggr_done = sem("stats_done"), sem("aggr_done")
        self.var_done, self.rstd_done, self.y_done = sem("var_done"), sem("rstd_done"), sem("y_done")
        self.turned, self.hi_done, self.lo_done = sem("turned"), sem("hi_done"), sem("lo_done")

    def dve_stats(self, e, k, src, tables_in, tables):
        nc = self.nc
        for t in range(TT):
            last = nc.vector.bn_stats(self.stats[:, t, :], src[:, t, :])
        last.then_inc(self.stats_done, 1)
        e.wait_ge(tables_in, tables)
        e.wait_ge(self.stats_done, k + 1)
        for t in range(TT):
            last = nc.vector.bn_aggr(self.mean_var[:, t, :], self.stats[:, t, :])
        last.then_inc(self.aggr_done, 1)
        e.wait_ge(self.aggr_done, k + 1)
        nc.vector.tensor_scalar(self.var[:, :], self.mean_var[:, :, 1], EPS, None, ALU.add)\
            .then_inc(self.var_done, 1)

    def dve_apply(self, e, k, src):
        nc = self.nc
        e.wait_ge(self.rstd_done, k + 1)
        e.wait_ge(self.turned, DC * k)
        for t in range(TT):
            last = nc.vector.tensor_scalar(self.y[:, t, :], src[:, t, :], self.mean_var[:, t, 0:1],
                                           self.rstd[:, t:t + 1], ALU.subtract, ALU.mult)
        last.then_inc(self.y_done, 1)

    def pool_rstd(self, e, k, minus_half):
        e.wait_ge(self.var_done, k + 1)
        self.nc.gpsimd.tensor_tensor(self.rstd[:, :], self.var[:, :], minus_half, ALU.pow)\
            .then_inc(self.rstd_done, 1)

    def pe_turn(self, e, k, banks, ident):
        e.wait_ge(self.y_done, k + 1)
        for c in range(DC):
            for t in range(TT):
                last = self.nc.tensor.transpose(banks[c][:, t * P:(t + 1) * P],
                                                self.y[:, t, c * P:(c + 1) * P], ident)
            last.then_inc(self.turned, 1)

    def act_hi(self, e, k, banks, hi, chunks=range(DC)):
        for c in chunks:
            e.wait_ge(self.turned, DC * k + c + 1)
            self.nc.scalar.activation(hi(c), banks[c][:, :], ACT.Copy).then_inc(self.hi_done, 1)

    def dve_lo(self, e, k, banks, hi, lo, chunks=range(DC)):
        for c in chunks:
            e.wait_ge(self.hi_done, DC * k + c + 1)
            self.nc.vector.tensor_tensor(lo(c), banks[c][:, :], hi(c).bitcast(F32), ALU.subtract)\
                .then_inc(self.lo_done, 1)


def build(nc, x, wq, wk, wv, wo, su_ug, su_dp, ws_ug, ws_dp, w_up, w_gate, w_down,
          c_ident, c_had, c_bias, out):
    x2_d = nc.dram_tensor("x2_scratch", [T, D], F32).ap()
    z_d = nc.dram_tensor("z_scratch", [HP, 2, DH, T], F32).ap()
    wug_d = nc.dram_tensor("wug_scratch", [P, 2 * DC * 2 * INTER], F32).ap()
    wdn_d = nc.dram_tensor("wdn_scratch", [P, 2 * JC * D], F32).ap()
    group_view = "(g t p) d -> g p t d"
    x_g = x.rearrange("b s d -> (b s) d").rearrange(group_view, g=G, p=P)
    x2_g = x2_d.rearrange(group_view, g=G, p=P)
    out_g = out.rearrange("b s d -> (b s) d").rearrange(group_view, g=G, p=P)

    whole = ExitStack()
    with whole:
        psum = [whole.enter_context(nc.psum_tensor(f"bank{i}", [P, 1024], F32)) for i in range(4)]
        bank = [psum[i // 2][:, i % 2 * 512:i % 2 * 512 + 512] for i in range(8)]
        ident = whole.enter_context(nc.sbuf_tensor("ident", [P, P], F32))
        minus_half = whole.enter_context(nc.sbuf_tensor("minus_half", [P, TT], F32))
        bias = whole.enter_context(nc.sbuf_tensor("bias", [P, 2, S], F32))
        shared = whole.enter_context(nc.sbuf_tensor("tokens_or_wo", [P, 2, DC * T], F32R))
        wo_t = shared[:, :, :].rearrange("p a (h o) -> p a h o", h=H)
        tok_t = shared[:, :, :].rearrange("p a (c t) -> p a c t", c=DC)
        w_raw = whole.enter_context(nc.sbuf_tensor("w_raw", [P, 3, 2, D], F32))
        w_or_z = whole.enter_context(nc.sbuf_tensor("weights_or_z", [P, 2 * 4 * GT], F32R))
        w_t = w_or_z[:, 0:3 * 2 * DC * 2 * DH].rearrange("p (m a c n) -> p m a c n", m=3, a=2, c=DC)
        z_raw = w_or_z[:, :].bitcast(F32).rearrange("p (a h t) -> p a h t", a=2, h=4)
        sem = lambda n: whole.enter_context(nc.semaphore(n))
        tables_in, halves_set, x_in, w_in = sem("tables_in"), sem("halves_set"), sem("x_in"), sem("w_in")
        z_sb = whole.enter_context(nc.sbuf_tensor("z_sb", [P, 2, GT], F32))
        z_in, z_out = [sem("z_in0"), sem("z_in1")], [sem("z_out0"), sem("z_out1")]
        TABLES = 16 * 2

        w_v = [w.rearrange("(a h p) d -> a p h d", h=2, p=P) for w in (wq, wk, wv)]

        def load_w(sp, hp):
            for m in range(3):
                sp.dma_start(w_raw[:, m, :, :], w_v[m][hp]).then_inc(w_in, 16)

        def load_heads(sp, g, c):
            for i in range(2):
                sp.dma_start(z_raw[:, c % 2, 2 * i:2 * i + 2, :],
                             z_d[2 * c + i, :, :, bass.ds(g * GT, GT)].rearrange("h p t -> p h t"))\
                    .then_inc(z_in[c % 2], 16)

        with ExitStack() as ctx:
            w_ug = ctx.enter_context(nc.sbuf_tensor("w_ug", [P, 2, DC, 2 * INTER], F32R))
            w_dn = ctx.enter_context(nc.sbuf_tensor("w_dn", [P, 2, JC, D], F32R))
            r = ctx.enter_context(nc.sbuf_tensor("f1_r", [P, TT, D], F32))
            ln = LayerNorm(nc, ctx, "f1_ln")
            with ExitStack() as scratch:
                prepare(nc, scratch, bank, w_up, w_gate, w_down, su_ug, su_dp, ws_ug, ws_dp,
                        c_ident, c_had, c_bias, ident, bias, minus_half, w_ug, w_dn,
                        tables_in, TABLES, halves_set, x_g[0], x_in, r, ln)
            with ExitStack() as work:
                ffn(nc, work, 1, bank, x_g, x2_g, w_ug, w_dn, ident, minus_half, tables_in, TABLES,
                    r, x_in, ln, tok_t=tok_t, load_w=load_w, w_in=w_in, w_raw=w_raw, w_t=w_t,
                    spills=[(wug_d, w_ug[:, :, :, :].rearrange("p a c n -> p (a c n)")),
                            (wdn_d, w_dn[:, :, :, :].rearrange("p a c n -> p (a c n)"))])
        with ExitStack() as work:
            attention(nc, work, psum, bank, wo, z_d, tok_t, wo_t, w_raw, w_t, w_in, load_w, load_heads,
                      z_sb, z_out, bias, ident)
        with ExitStack() as ctx:
            w_ug = ctx.enter_context(nc.sbuf_tensor("w_ug_back", [P, 2, DC, 2 * INTER], F32R))
            w_dn = ctx.enter_context(nc.sbuf_tensor("w_dn_back", [P, 2, JC, D], F32R))
            r = ctx.enter_context(nc.sbuf_tensor("f2_r", [P, TT, D], F32))
            ln = LayerNorm(nc, ctx, "f2_ln")
            x2_in = ctx.enter_context(nc.semaphore("x2_in"))
            ffn(nc, ctx, 2, bank, x2_g, out_g, w_ug, w_dn, ident, minus_half, tables_in, TABLES,
                r, x2_in, ln, wo_t=wo_t, z_raw=z_raw, z_in=z_in, z_out=z_out,
                load_heads=load_heads,
                loads=[(wug_d[:, w * DC * 2 * INTER:(w + 1) * DC * 2 * INTER],
                        w_ug[:, w, :, :].rearrange("p c n -> p (c n)")) for w in (HI, LO)] + [
                       (wdn_d, w_dn[:, :, :, :].rearrange("p a c n -> p (a c n)"))])


def prepare(nc, ctx, bank, w_up, w_gate, w_down, su_ug, su_dp, ws_ug, ws_dp,
            c_ident, c_had, c_bias, ident, bias, minus_half, w_ug, w_dn,
            tables_in, TABLES, halves_set, x_group, x_in, r, ln):
    sb = lambda n, shape, dt=F32: ctx.enter_context(nc.sbuf_tensor(n, shape, dt))
    sem = lambda n: ctx.enter_context(nc.semaphore(n))
    had_f, scrap = sb("had_f", [P, 2, P]), sb("scrap", [P, TT])
    had = sb("had", [P, 2, P], F32R)
    VECS = [(ws_ug, 2 * JC), (ws_dp, DC), (su_ug, DC), (su_dp, JC)]
    NV = sum(rows for _, rows in VECS)
    vec_rows, vec = sb("vec_rows", [NV, P]), sb("vec", [P, NV])
    row_ug, row_dn = vec[:, 0:2 * JC], vec[:, 2 * JC:2 * JC + DC]
    sign_ug, sign_dp = vec[:, 2 * JC + DC:2 * JC + 2 * DC], vec[:, 2 * JC + 2 * DC:NV]
    raw_ug = sb("raw_ug", [P, 2 * JC, D])
    raw_dn, sum_dn = sb("raw_dn", [P, DC, INTER]), sb("sum_dn", [P, DC, INTER])
    ugT = sb("ugT", [P, 2, DC, 2 * INTER], F32R)
    dnT = sb("dnT", [P, 2, JC, D], F32R)
    vec_in, dn_in = sem("vec_in"), sem("dn_in")
    ug_in = [sem(f"ug_in{n}") for n in range(4)]
    had_in, had_done = sem("had_in"), sem("had_done")
    vec_turned, vec_done = sem("vec_turned"), sem("vec_done")
    pool_rows, act_rows, dve_summed, pool_summed = (
        sem("pool_rows"), sem("act_rows"), sem("dve_summed"), sem("pool_summed"))
    ps_done, hi_done, lo_done = sem("ps_done"), sem("hi_done"), sem("lo_done")

    JG = 4
    units = []

    def add(kind, *ab):
        units.append((kind, *ab))
    for g in range(JG):
        for c in range(DC):
            add("turn_ug", g, c)
        if g >= 1:
            for c in range(DC):
                add("had_ug", g - 1, c)
    for n in range(JC // 2):
        add("turn_dn", n, 0)
    for c in range(DC):
        add("had_ug", JG - 1, c)
    for n in range(JC):
        add("had_dn", n, 0)
    order = {u: n for n, u in enumerate(units)}

    def parts(u):
        kind, a, b = u
        if kind == "turn_ug":
            return 512, [ugT[:, w, b, a * 512:(a + 1) * 512] for w in (HI, LO)], None
        if kind == "had_ug":
            return 512, [w_ug[:, w, b, a * 512:(a + 1) * 512] for w in (HI, LO)], sign_ug[:, b:b + 1]
        if kind == "turn_dn":
            return 512, [dnT[:, w, 2 * a:2 * a + 2, :].rearrange("p c o -> p (c o)") for w in (HI, LO)], None
        return D, [w_dn[:, w, a, :] for w in (HI, LO)], sign_dp[:, a:a + 1]

    ROWS_AT = {0: [0, 1], 2: [2], 4: [3]}

    def load_vecs(e, first, end):
        for source, rows in VECS[first:end]:
            row = sum(n for _, n in VECS[:[v for v, _ in VECS].index(source)])
            e.dma_start(vec_rows[row:row + rows, :], source.rearrange("(c p) -> c p", p=P))\
                .then_inc(vec_in, 16)

    def butterfly(engine, done, src, dst, h):
        a, b = (x[:, :, :].rearrange("p c (a b k) -> p (c a) b k", b=2, k=h * P) for x in (src, dst))
        engine.tensor_tensor(b[:, :, 0, :], a[:, :, 0, :], a[:, :, 1, :], ALU.add)
        engine.tensor_tensor(b[:, :, 1, :], a[:, :, 0, :], a[:, :, 1, :], ALU.subtract).then_inc(done, 1)

    block = ctx.enter_context(nc.Block())

    @block.sync
    def _(sp):
        up_v = w_up.rearrange("(c p) d -> p c d", p=P)
        gate_v = w_gate.rearrange("(c p) d -> p c d", p=P)
        sp.dma_start(ident[:, :], c_ident).then_inc(tables_in, 16)
        load_vecs(sp, 2, 4)
        sp.dma_start(raw_ug[:, 0:4, :], up_v[:, 0:4, :]).then_inc(ug_in[0], 16)
        sp.dma_start(raw_ug[:, 4:8, :], up_v[:, 4:8, :]).then_inc(ug_in[1], 16)
        sp.dma_start(raw_dn[:, :, :], w_down.rearrange("(c p) n -> p c n", p=P)).then_inc(dn_in, 16)
        sp.dma_start(raw_ug[:, 8:12, :], gate_v[:, 0:4, :]).then_inc(ug_in[2], 16)
        sp.dma_start(r[:, :, :], x_group).then_inc(x_in, 16)
        sp.dma_start(raw_ug[:, 12:16, :], gate_v[:, 4:8, :]).then_inc(ug_in[3], 16)
        sp.wait_ge(tables_in, 16)
        sp.dma_start(bias[:, :, :], c_bias).then_inc(tables_in, 16)

    @block.gpsimd
    def _(pool):
        nc.gpsimd.memset(minus_half[:, :], -0.5).then_inc(halves_set, 1)
        pool.wait_ge(vec_done, 3)
        for g in range(JG):
            pool.wait_ge(ug_in[g], 16)
            for n in range(4 * g, 4 * g + 2):
                nc.gpsimd.tensor_scalar(raw_ug[:, n, :], raw_ug[:, n, :], row_ug[:, n:n + 1], 1.0,
                                        ALU.mult, ALU.mult).then_inc(pool_rows, 1)
        pool.wait_ge(halves_set, 1)
        ln.pool_rstd(pool, 0, minus_half[:, :])
        pool.wait_ge(dve_summed, 2)
        butterfly(nc.gpsimd, pool_summed, raw_dn, sum_dn, 1)

    @block.tensor
    def _(pe):
        pe.wait_ge(tables_in, 16)
        pe.wait_ge(vec_in, 64)
        nc.tensor.transpose(bank[7][:, 0:NV], vec_rows[:, :], ident[0:NV, 0:NV]).then_inc(vec_turned, 1)
        for n, (kind, a, b) in enumerate(units):
            ps = bank[n % 8]
            if n == 7:
                pe.wait_ge(vec_done, 3)
            if n >= 8:
                pe.wait_ge(lo_done, n - 7)
            if kind == "turn_ug":
                pe.wait_ge(pool_rows, 2 * (a + 1))
                pe.wait_ge(act_rows, 2 * (a + 1) + (DC if a >= 2 else 0))
                for t in range(4):
                    last = nc.tensor.transpose(ps[:, t * P:(t + 1) * P],
                                               raw_ug[:, 4 * a + t, b * P:(b + 1) * P], ident[:, :])
            elif kind == "turn_dn":
                pe.wait_ge(pool_summed, 1)
                for i in range(2):
                    for c in range(DC):
                        last = nc.tensor.transpose(ps[:, (2 * i + c) * P:(2 * i + c + 1) * P],
                                                   sum_dn[:, c, (2 * a + i) * P:(2 * a + i + 1) * P],
                                                   ident[:, :])
            elif kind == "had_ug":
                pe.wait_ge(had_done, 1)
                pe.wait_ge(lo_done, order["turn_ug", a, DC - 1] + 1)
                for c in range(DC):
                    for w in (HI, LO):
                        last = nc.tensor.matmul(ps, had[:, b * c % 2, :],
                                                ugT[:, w, c, a * 512:(a + 1) * 512],
                                                start=(c == 0 and w == HI), stop=(c == DC - 1 and w == LO))
            else:
                pe.wait_ge(lo_done, order["turn_dn", a // 2, 0] + 1)
                for w in (HI, LO):
                    last = nc.tensor.matmul(ps[:, 0:D], had[:, 0, :], dnT[:, w, a, :],
                                            start=(w == HI), stop=(w == LO))
            last.then_inc(ps_done, 1)

    @block.scalar
    def _(act):
        load_vecs(act, 0, 2)
        act.dma_start(had_f[:, :, :], c_had).then_inc(had_in, 16)
        act.wait_ge(halves_set, 1)
        nc.scalar.activation(scrap[:, :], minus_half[:, :], ACT.Copy)
        act.wait_ge(vec_done, 3)
        for n, u in enumerate(units):
            if n == 2:
                act.wait_ge(dn_in, 16)
                for c in range(DC):
                    nc.scalar.activation(raw_dn[:, c, :], raw_dn[:, c, :], ACT.Copy,
                                         scale=row_dn[:, c:c + 1]).then_inc(act_rows, 1)
            if n in ROWS_AT:
                for g in ROWS_AT[n]:
                    act.wait_ge(ug_in[g], 16)
                    for t in range(2, 4):
                        nc.scalar.activation(raw_ug[:, 4 * g + t, :], raw_ug[:, 4 * g + t, :], ACT.Copy,
                                             scale=row_ug[:, 4 * g + t:4 * g + t + 1]).then_inc(act_rows, 1)
            cols, place, sign = parts(u)
            act.wait_ge(ps_done, n + 1)
            nc.scalar.activation(place[HI], bank[n % 8][:, 0:cols], ACT.Copy,
                                 scale=1.0 if sign is None else sign).then_inc(hi_done, 1)

    @block.vector
    def _(dve):
        dve.wait_ge(vec_turned, 1)
        turned, ug, dp = bank[7], 2 * JC + DC, 2 * JC + 2 * DC
        nc.vector.tensor_copy(vec[:, 0:ug], turned[:, 0:ug]).then_inc(vec_done, 1)
        nc.vector.tensor_scalar(sign_ug, turned[:, ug:dp], D ** -0.5 / FFN_SCALE * FFN_SCALE, None,
                                ALU.mult).then_inc(vec_done, 1)
        nc.vector.tensor_scalar(sign_dp, turned[:, dp:NV],
                                0.5 * INTER ** -0.5 / FFN_SCALE * FFN_SCALE, None,
                                ALU.mult).then_inc(vec_done, 1)
        dve.wait_ge(had_in, 16)
        nc.vector.tensor_copy(had[:, :, :], had_f[:, :, :]).then_inc(had_done, 1)
        dve.wait_ge(vec_done, 3)
        for n, u in enumerate(units):
            cols, place, sign = parts(u)
            dve.wait_ge(hi_done, n + 1)
            hi = place[HI].bitcast(F32)
            if sign is None:
                last = nc.vector.tensor_tensor(place[LO], bank[n % 8][:, 0:cols], hi, ALU.subtract)
            else:
                last = nc.vector.scalar_tensor_tensor(place[LO], bank[n % 8][:, 0:cols], sign, hi,
                                                      ALU.mult, ALU.subtract)
            last.then_inc(lo_done, 1)
            if n == 1:
                dve.wait_ge(act_rows, 2 * 2 + DC)
                butterfly(nc.vector, dve_summed, raw_dn, sum_dn, 4)
            if n == 3:
                dve.wait_ge(x_in, 16)
                ln.dve_stats(dve, 0, r, had_in, 16)
                dve.wait_ge(dve_summed, 1)
                butterfly(nc.vector, dve_summed, sum_dn, raw_dn, 2)
            if n == 7:
                ln.dve_apply(dve, 0, r)


def ffn(nc, ctx, phase, bank, src_g, dst_g, w_ug, w_dn, ident, minus_half, tables_in, TABLES,
        r, src_in, ln, tok_t=None, load_w=None, w_in=None, w_raw=None, w_t=None, spills=(),
        wo_t=None, z_raw=None, z_in=None, z_out=None, load_heads=None, loads=()):
    sb = lambda n, shape, dt=F32: ctx.enter_context(nc.sbuf_tensor(f"f{phase}_{n}", shape, dt))
    sem = lambda n: ctx.enter_context(nc.semaphore(f"f{phase}_{n}"))
    first_phase = phase == 1
    res = sb("res", [P, TT, D])
    yT = sb("yT", [P, 2, DC, GT], F32R)
    silu = sb("silu", [P, 2, GT])
    hid = sb("hid", [P, 2, GT])
    hidT = sb("hidT", [P, 4, 2, GT], F32R)
    dst = sb("dst", [P, TT, D])
    gate_ps, up_ps, down_ps, pre_ps = bank[0:2], bank[2:4], bank[4:6], bank[6:8]
    ln2 = LayerNorm(nc, ctx, "f1_ln2") if first_phase else None
    weights_in, spilled = [sem("wug_in"), sem("wdn_in")], sem("spilled")
    gu_done, silu_done, hid_done = sem("gu_done"), sem("silu_done"), sem("hid_done")
    hi_done, lo_done, down_done = sem("hi_done"), sem("lo_done"), sem("down_done")
    dst_done, dst_out, res_done = sem("dst_done"), sem("dst_out"), sem("res_done")
    pool_taken = sem("pool_taken")
    if not first_phase:
        src = sb("src", [P, TT, D])
        z_t = sb("z_t", [P, 8, 2, GT], F32R)
        zhi_done, zlo_done, oproj_done, r_done = (
            sem("zhi_done"), sem("zlo_done"), sem("oproj_done"), sem("r_done"))
    else:
        w_turned, whi_done, wlo_done = sem("w_turned"), sem("whi_done"), sem("wlo_done")
    HEADS = {0: range(0, 6), 1: range(6, 11), 2: range(11, 16)}
    EARLY = range(0, 4)
    HEADS_1 = {0: range(4, 10), 1: range(10, 16)}
    first_ps = pre_ps if first_phase else down_ps

    def heads(g, j):
        return [] if first_phase else (HEADS_1 if isinstance(g, int) and g == 0 else HEADS).get(j, [])


    block = ctx.enter_context(nc.Block())

    def run(e, engine_body):
        engine_body(0, False, True)
        with e.Fori(1, G - 1) as g:
            engine_body(g, first_phase, True)
        engine_body(G - 1, first_phase, False)

    @block.sync
    def _(sp):
        if not first_phase:
            sp.dma_start(src[:, :, :], src_g[0]).then_inc(src_in, 16)
            for stored in z_out:
                sp.wait_ge(stored, 16 * 2 * B * HP)
            for c in range(2, 4):
                sp.wait_ge(zlo_done, 4 * c - 4)
                load_heads(sp, 0, c)
            for n, (d, s) in enumerate(loads):
                sp.dma_start(s.bitcast(F32), d).then_inc(weights_in[n // 2], 16)
                if n == HI:
                    sp.wait_ge(zlo_done, 12)
                    load_heads(sp, 1, 0)
        if first_phase:
            load_w(sp, 0)
        for d, s in spills:
            sp.dma_start(d, s.bitcast(F32)).then_inc(spilled, 16)

        def body(g, post, nxt):
            if nxt and first_phase:
                sp.wait_ge(res_done, g + 1)
                sp.dma_start(r[:, :, :], src_g[g + 1]).then_inc(src_in, 16)
            if nxt and not first_phase:
                sp.wait_ge(r_done, g + 1)
                sp.dma_start(src[:, :, :], src_g[g + 1]).then_inc(src_in, 16)
                for c in range(1 if isinstance(g, int) and g == 0 else 0, 4):
                    sp.wait_ge(zlo_done, H * g + 12 + 4 * c)
                    load_heads(sp, g + 1, c)
        run(sp, body)
        sp.wait_ge(dst_out, 16 * G)
        if spills:
            sp.wait_ge(spilled, 16 * len(spills))

    @block.gpsimd
    def _(pool):
        if not first_phase:
            ln.pool_rstd(pool, 0, minus_half[:, :])

        def body(g, post, nxt):
            pool.wait_ge(ln.y_done, g + 1)
            if not (isinstance(g, int) and g == 0):
                pool.wait_ge(dst_done, g)
            pool.sem_inc(pool_taken, 1)
            nc.gpsimd.tensor_copy(res[:, :, :], r[:, :, :]).then_inc(res_done, 1)
            if post:
                ln2.pool_rstd(pool, g - 1, minus_half[:, :])
            if nxt:
                ln.pool_rstd(pool, g + 1, minus_half[:, :])
        run(pool, body)
        if first_phase:
            ln2.pool_rstd(pool, G - 1, minus_half[:, :])

    @block.tensor
    def _(pe):
        def up_gate(g, j, n):
            if not isinstance(n, int) or n >= 2:
                pe.wait_ge(hid_done, n - 1)
            if j == 0:
                pe.wait_ge(ln.lo_done, DC * (g + 1))
            for out_ps, first_col in ((gate_ps, INTER), (up_ps, 0)):
                for c in range(DC):
                    cols = slice(first_col + j * P, first_col + (j + 1) * P)
                    last = mm3(nc, out_ps[j % 2], [w_ug[:, w, c, cols] for w in (HI, LO)],
                               [yT[:, w, c, :] for w in (HI, LO)], c == 0, c == DC - 1)
            last.then_inc(gu_done, 1)

        def down(g, j, n):
            if loads and isinstance(n, int) and n == 0:
                pe.wait_ge(weights_in[1], 16)
            pe.wait_ge(lo_done, n + 1)
            if j == 0 and not (isinstance(g, int) and g == 0):
                pe.wait_ge(dst_done, g)
            for t in range(TT):
                last = mm3(nc, down_ps[t // 2][:, t % 2 * D:(t % 2 + 1) * D],
                           [hidT[:, j % 4, w, t * P:(t + 1) * P] for w in (HI, LO)],
                           [w_dn[:, w, j, :] for w in (HI, LO)],
                           j == 0 and t % 2 == 0, j == JC - 1, skip_group_check=True)
            last.then_inc(down_done, 1)

        def oproj(g, heads):
            for h in heads:
                if h == 0 and isinstance(g, int) and g == 1:
                    pe.wait_ge(r_done, 1)
                elif h == 0 and not (isinstance(g, int) and g == 0):
                    pe.wait_ge(ln.lo_done, DC * g)
                pe.wait_ge(zlo_done, H * g + h + 1)
                for t in range(TT):
                    last = mm3(nc, pre_ps[t // 2][:, t % 2 * D:(t % 2 + 1) * D],
                               [z_t[:, h % 8, w, t * P:(t + 1) * P] for w in (HI, LO)],
                               [wo_t[:, w, h, :] for w in (HI, LO)],
                               h == 0 and t % 2 == 0, h == H - 1, skip_group_check=True)
                last.then_inc(oproj_done, 1)

        if not first_phase:
            oproj(0, range(H))
            oproj(1, EARLY)
        ln.pe_turn(pe, 0, first_ps, ident[:, :])
        if loads:
            pe.wait_ge(weights_in[0], 32)
        up_gate(0, 0, 0)
        up_gate(0, 1, 1)

        def body(g, post, nxt):
            for j in range(JC - 2):
                down(g, j, JC * g + j)
                up_gate(g, j + 2, JC * g + j + 2)
                if nxt:
                    oproj(g + 1, heads(g, j))
                if post and j == 1:
                    ln2.pe_turn(pe, g - 1, pre_ps, ident[:, :])
            if nxt:
                if post:
                    pe.wait_ge(ln2.lo_done, DC * g)
                ln.pe_turn(pe, g + 1, pre_ps, ident[:, :])
            for j in range(JC - 2, JC):
                down(g, j, JC * g + j)
            if nxt:
                for j in range(2):
                    up_gate(g + 1, j, JC * (g + 1) + j)
        run(pe, body)
        if first_phase:
            pe.wait_ge(w_in, 16 * 3)
            pe.wait_ge(hid_done, JC * G)
            for m in range(3):
                for c in range(DC):
                    for h in range(2):
                        last = nc.tensor.transpose(bank[m][:, (2 * c + h) * P:(2 * c + h + 1) * P],
                                                   w_raw[:, m, h, c * P:(c + 1) * P], ident[:, :])
                last.then_inc(w_turned, 1)
            ln2.pe_turn(pe, G - 1, pre_ps, ident[:, :])

    def w_place(m, w):
        return w_t[:, m, w, :, :].rearrange("p c n -> p (c n)")

    yT_hi, yT_lo = (lambda c: yT[:, HI, c, :]), (lambda c: yT[:, LO, c, :])

    def tok(w, g):
        return lambda c: tok_t[:, w, c, bass.ds(g * GT, GT)]

    @block.scalar
    def _(act):
        def silu_of(j, n):
            act.wait_ge(gu_done, n + 1)
            nc.scalar.activation(silu[:, j % 2, :], gate_ps[j % 2], ACT.Silu).then_inc(silu_done, 1)

        def hid_hi(j, n):
            act.wait_ge(hid_done, n + 1)
            if not isinstance(n, int) or n >= 4:
                act.wait_ge(down_done, n - 3)
            nc.scalar.activation(hidT[:, j % 4, HI, :], hid[:, j % 2, :], ACT.Copy).then_inc(hi_done, 1)

        def z_hi(g, heads):
            for h in heads:
                act.wait_ge(z_in[h // 4 % 2], 32 * 2 * g + 32 * (h // 8 + 1))
                if not (isinstance(g, int) and g == 0 and h < 8):
                    act.wait_ge(oproj_done, H * g + h - 7)
                nc.scalar.activation(z_t[:, h % 8, HI, :], z_raw[:, h // 4 % 2, h % 4, :], ACT.Copy)\
                    .then_inc(zhi_done, 1)

        if not first_phase:
            z_hi(0, range(H))
            z_hi(1, EARLY)
        ln.act_hi(act, 0, first_ps, yT_hi)
        for j in range(2):
            silu_of(j, j)
            hid_hi(j, j)

        def tok_hi(k):
            for c in range(DC):
                act.wait_ge(ln2.turned, DC * k + c + 1)
                nc.scalar.activation(tok(HI, k)(c), pre_ps[c], ACT.Copy).then_inc(ln2.hi_done, 1)

        def store(g):
            act.wait_ge(dst_done, g + 1)
            act.dma_start(dst_g[g], dst[:, :, :]).then_inc(dst_out, 16)

        def body(g, post, nxt):
            if not (isinstance(g, int) and g == 0):
                store(g - 1)
            for j in range(JC - 2):
                if nxt:
                    z_hi(g + 1, heads(g, j))
                silu_of(j + 2, JC * g + j + 2)
                if nxt and j == JC - 3:
                    ln.act_hi(act, g + 1, pre_ps, yT_hi, [0])
                hid_hi(j + 2, JC * g + j + 2)
                if post and j == 2:
                    tok_hi(g - 1)
            if nxt:
                ln.act_hi(act, g + 1, pre_ps, yT_hi, [1])
                for j in range(2):
                    silu_of(j, JC * (g + 1) + j)
                    hid_hi(j, JC * (g + 1) + j)
        run(act, body)
        store(G - 1)
        if first_phase:
            for m in range(3):
                act.wait_ge(w_turned, m + 1)
                nc.scalar.activation(w_place(m, HI), bank[m], ACT.Copy).then_inc(whi_done, 1)
            tok_hi(G - 1)

    @block.vector
    def _(dve):
        def hid_of(j, n):
            dve.wait_ge(silu_done, n + 1)
            nc.vector.tensor_tensor(hid[:, j % 2, :], up_ps[j % 2], silu[:, j % 2, :], ALU.mult)\
                .then_inc(hid_done, 1)

        def hid_lo(j, n):
            dve.wait_ge(hi_done, n + 1)
            nc.vector.tensor_tensor(hidT[:, j % 4, LO, :], hid[:, j % 2, :],
                                    hidT[:, j % 4, HI, :].bitcast(F32), ALU.subtract).then_inc(lo_done, 1)

        def z_lo(g, heads):
            for h in heads:
                dve.wait_ge(zhi_done, H * g + h + 1)
                nc.vector.tensor_tensor(z_t[:, h % 8, LO, :], z_raw[:, h // 4 % 2, h % 4, :],
                                        z_t[:, h % 8, HI, :].bitcast(F32), ALU.subtract)\
                    .then_inc(zlo_done, 1)

        def residual(g):
            dve.wait_ge(oproj_done, H * (g + 1))
            dve.wait_ge(src_in, 16 * (g + 1))
            if not (isinstance(g, int) and g == 0):
                dve.wait_ge(res_done, g)
            for t in range(0, TT, 2):
                last = nc.vector.tensor_tensor(r[:, t:t + 2, :].rearrange("p t d -> p (t d)"),
                                               pre_ps[t // 2],
                                               src[:, t:t + 2, :].rearrange("p t d -> p (t d)"), ALU.add)
            last.then_inc(r_done, 1)
            dve.wait_ge(r_done, g + 1)

        def stats(g):
            if first_phase:
                dve.wait_ge(src_in, 16 * (g + 1))
            else:
                residual(g)
            ln.dve_stats(dve, g, r, tables_in, TABLES)

        def finish(g):
            dve.wait_ge(down_done, JC * (g + 1))
            dve.wait_ge(res_done, g + 1)
            if not (isinstance(g, int) and g == 0):
                dve.wait_ge(dst_out, 16 * g)
            for t in range(0, TT, 2):
                last = nc.vector.tensor_tensor(dst[:, t:t + 2, :].rearrange("p t d -> p (t d)"),
                                               down_ps[t // 2],
                                               res[:, t:t + 2, :].rearrange("p t d -> p (t d)"), ALU.add)
            last.then_inc(dst_done, 1)

        if not first_phase:
            z_lo(0, range(H))
            z_lo(1, EARLY)
            stats(0)
            ln.dve_apply(dve, 0, r)
        ln.dve_lo(dve, 0, first_ps, yT_hi, yT_lo)
        for j in range(2):
            hid_of(j, j)
            hid_lo(j, j)

        def body(g, post, nxt):
            for j in range(JC - 2):
                if post and j == 0:
                    dve.wait_ge(dst_done, g)
                    ln2.dve_stats(dve, g - 1, dst, tables_in, TABLES)
                if nxt:
                    z_lo(g + 1, heads(g, j))
                hid_of(j + 2, JC * g + j + 2)
                if post and j == 0:
                    ln2.dve_apply(dve, g - 1, dst)
                if nxt and j == 4:
                    ln.dve_apply(dve, g + 1, r)
                if nxt and j == JC - 3:
                    ln.dve_lo(dve, g + 1, pre_ps, yT_hi, yT_lo, [0])
                hid_lo(j + 2, JC * g + j + 2)
                if post and j == 2:
                    ln2.dve_lo(dve, g - 1, pre_ps, tok(HI, g - 1), tok(LO, g - 1))
                if nxt and j == 3:
                    stats(g + 1)
            if nxt:
                ln.dve_lo(dve, g + 1, pre_ps, yT_hi, yT_lo, [1])
            finish(g)
            if nxt:
                for j in range(2):
                    hid_of(j, JC * (g + 1) + j)
                    hid_lo(j, JC * (g + 1) + j)
        run(dve, body)
        if first_phase:
            dve.wait_ge(dst_done, G)
            ln2.dve_stats(dve, G - 1, dst, tables_in, TABLES)
            ln2.dve_apply(dve, G - 1, dst)
            for m in range(3):
                dve.wait_ge(whi_done, m + 1)
                nc.vector.tensor_tensor(w_place(m, LO), bank[m], w_place(m, HI).bitcast(F32),
                                        ALU.subtract).then_inc(wlo_done, 1)
            ln2.dve_lo(dve, G - 1, pre_ps, tok(HI, G - 1), tok(LO, G - 1))


def attention(nc, ctx, psum, bank, wo, z_d, tok_t, wo_t, w_raw, w_t, w_in, load_w, load_heads,
              z_sb, z_out, bias, ident):
    sb = lambda n, shape, dt=F32: ctx.enter_context(nc.sbuf_tensor(n, shape, dt))
    sem = lambda n: ctx.enter_context(nc.semaphore(n))
    ST = 2 * B
    NU = ST * QT
    QG = QT // 2
    q_t = sb("q_t", [P, 2, 2, S], F32R)
    k_t = sb("k_t", [P, 2, 2, S], F32R)
    v = sb("v", [P, B, 2, QT, 2 * DH], F32R)
    prob = sb("prob", [P, QT * (QT + 1) // 2 * P])
    p_t = [sb("p_t0", [P, 2, QG, GT], F32R),
           sb("p_t1", [P, 2, QT, GT], F32R)]
    minus_max, row_sum, inv_sum = sb("minus_max", [P, QT]), sb("row_sum", [P, QT]), sb("inv_sum", [P, QT])
    turn_ps, z_ps, item_ps = bank[4:6], bank[6], bank[7]
    wo_in = [sem(f"wo_in{n}") for n in range(3)]
    s_done, clip_done, b_done = sem("s_done"), sem("clip_done"), sem("biased_done")
    exp_done, inv_done, norm_done = sem("exp_done"), sem("inv_done"), sem("norm_done")
    t_done, thi_done, tlo_done = sem("turned_done"), sem("thi_done"), sem("tlo_done")
    pv_done, z_done = sem("pv_done"), sem("z_done")
    item_done, ihi_done, ilo_done = sem("item_done"), sem("ihi_done"), sem("ilo_done")
    halved = sem("bias_halved")
    pool_taken, dve_taken = sem("pool_taken"), sem("dve_taken")
    WQ, WK, WV = range(3)

    WO_STEP = 3 * QT
    START = [("q", 0, 0), ("k", 0, 0), ("q", 0, 1), ("k", 0, 1)]
    START += [("v", 0, n) for n in range(QT // 2)]

    def items(nxt):
        found = []
        for s in range(ST):
            for n, kind in enumerate([("q", 0), ("k", 0), ("q", 1), ("k", 1)]):
                item = (kind[0], (s + 1) % ST, kind[1])
                if s < ST - 1:
                    found.append((QT * s + 1 + n, item))
                elif nxt:
                    found.append((QT * s + 2 + n, item))
            for n in range(2):
                if s < 2 or nxt:
                    found.append((QT * s + 6 + n, ("v", 1 if s < 2 else 0, 2 * (s % 2) + n)))
        if not nxt:
            found += [(WO_STEP + n, ("o", n)) for n in range(H // 2)]
        if nxt:
            found += [(2 * QT, ("w", WV)), (3 * QT, ("w", WQ)), (3 * QT + 1, ("w", WK))]
        return sorted(found, key=lambda f: f[0])

    ITEMS = len(items(True))
    NS = len(START)

    def number(hp, item, nxt=True):
        at = [i for _, i in items(nxt)].index(item)
        return NS + ITEMS * hp + at + 1

    def width(i):
        return (i + 1) * P

    def at_s(i):
        return 256 if i == 4 else 0

    def turn_banks(i):
        return [range(0, min(i + 1, 4))] + ([range(4, i + 1)] if i >= 4 else [])

    TB = sum(len(turn_banks(i)) for i in range(QT))

    def turn_number(hp, s, i, n):
        return ST * TB * hp + TB * s + sum(len(turn_banks(x)) for x in range(i)) + n

    LAG = 5
    PIECES = [(QG + LAG + 1, 0, range(0, 2)), (QG + LAG + 2, 0, range(2, 4)),
              (QT + LAG + 1, 1, range(0, 2)), (QT + LAG + 2, 1, range(2, 4)),
              (QT + LAG + 3, 1, range(4, 8))]

    def is_first(hp):
        return isinstance(hp, int) and hp == 0

    def of_unit(hp, u, lag):
        v = u - lag
        if v >= NU or v < 0 and is_first(hp):
            return None
        return (hp - 1 if v < 0 else hp), v % NU // QT, v % QT

    def unit(hp, s, i):
        return NU * hp + QT * s + i

    def pieces(hp, u):
        found = []
        for step, g, tiles in PIECES:
            if (u - step) % QT == 0:
                s = (u - step) // QT
                if s < 0:
                    if is_first(hp):
                        continue
                    a, s = hp - 1, s + ST
                else:
                    a = hp
                if s >= ST:
                    continue
                found.append((a, s, g, tiles, tiles[0] == 0, tiles[-1] == (QG if g == 0 else QT) - 1))
        return found

    TAIL = PIECES[-1][0] - QT + 2

    def run(e, step):
        def iteration(hp, nxt):
            for u in range(NU + (0 if nxt else TAIL)):
                step(hp, u, nxt)
        iteration(0, True)
        with e.Fori(1, HP - 1) as hp:
            iteration(hp, True)
        iteration(HP - 1, False)

    def prob_of(i):
        return prob[:, i * (i + 1) // 2 * P:(i + 1) * (i + 2) // 2 * P]

    def turn_slot(s, i, n):
        return turn_number(0, s, i, n) % 2

    def places(what, w):
        if what[0] == "w":
            return w_t[:, what[1], w, :, :].rearrange("p c n -> p (c n)")
        if what[0] == "o":
            return wo_t[:, w, 2 * what[1]:2 * what[1] + 2, :].rearrange("p h o -> p (h o)")
        if what[0] in "qk":
            return (q_t if what[0] == "q" else k_t)[:, what[1] % 2, w, what[2] * GT:(what[2] + 1) * GT]
        return v[:, what[1], w, 2 * what[2]:2 * what[2] + 2, :].rearrange("p c n -> p (c n)")

    def scale_of(what):
        return DH ** -0.5 if what[0] == "q" else 1.0

    def turned_place(s, i, n, w):
        tiles = turn_banks(i)[n]
        q = i % QG * P
        return p_t[i // QG][:, w, tiles[0]:tiles[-1] + 1, q:q + P]

    def item_at(hp, u, nxt):
        at = items(nxt)
        return [(NS + ITEMS * hp + n, item) for n, (w, item) in enumerate(at) if w == u]

    block = ctx.enter_context(nc.Block())

    @block.sync
    def _(sp):
        wo_v = wo.rearrange("(c p) n -> p c n", p=P)

        def store_z(hp, u):
            for a, s, g, _, _, last in pieces(hp, u):
                if last:
                    sp.wait_ge(z_done, 2 * ST * a + 2 * s + g + 1)
                    first_col = s // 2 * S + g * GT
                    sp.dma_start(z_d[a, s % 2, :, first_col:first_col + GT], z_sb[:, g, :])\
                        .then_inc(z_out[g], 16)

        def step(hp, u, nxt):
            if u == 0 and nxt:
                if not is_first(hp):
                    sp.wait_ge(item_done, NS + ITEMS * hp)
                load_w(sp, hp + 1)
            if not nxt:
                for n in range(H // 2):
                    if u == (0 if n < 3 else WO_STEP + n - 2):
                        sp.wait_ge(item_done, NS + ITEMS * hp if n < 3 else number(hp, ("o", n - 3), nxt))
                        sp.dma_start(w_raw[:, n % 3, :, :], wo_v[:, :, n * 2 * DH:(n + 1) * 2 * DH])\
                            .then_inc(wo_in[n % 3], 16)
                if u == 3 * QT:
                    sp.wait_ge(ilo_done, number(hp, ("k", ST - 1, 1), nxt))
                    for g in range(2):
                        sp.wait_ge(z_out[g], 16 * ST * 4)
                    load_heads(sp, 0, 0)
                    load_heads(sp, 0, 1)
            store_z(hp, u)
        run(sp, step)

    @block.gpsimd
    def _(pool):
        def step(hp, u, nxt):
            f = of_unit(hp, u, 1)
            if f:
                a, s, i = f
                n = unit(a, s, i)
                pool.wait_ge(inv_done, n + 1)
                pool.sem_inc(pool_taken, 1)
                nc.gpsimd.tensor_scalar(prob_of(i), prob_of(i), inv_sum[:, i:i + 1], 1.0,
                                        ALU.mult, ALU.mult).then_inc(norm_done, 1)
            if u == 3 and not is_first(hp):
                halve(1, unit(hp, 0, 0))
            if u == 3 * QT + 3 and nxt:
                halve(0, unit(hp, 3, 0))

        def halve(head, used):
            pool.wait_ge(b_done, used)
            pool.sem_inc(pool_taken, 1)
            nc.gpsimd.tensor_scalar(bias[:, head, :], bias[:, head, :], 0.5, 1.0, ALU.mult, ALU.mult)\
                .then_inc(halved, 1)
        run(pool, step)

    @block.tensor
    def _(pe):
        def item(n, what, ps):
            if what[0] == "w":
                m = what[1]
                for c in range(DC):
                    for h in range(2):
                        last = nc.tensor.transpose(ps[:, (2 * c + h) * P:(2 * c + h + 1) * P],
                                                   w_raw[:, m, h, c * P:(c + 1) * P], ident[:, :])
            elif what[0] == "o":
                for i in range(2):
                    for c in range(DC):
                        last = nc.tensor.transpose(ps[:, (2 * i + c) * P:(2 * i + c + 1) * P],
                                                   w_raw[:, what[1] % 3, c, i * P:(i + 1) * P], ident[:, :])
            elif what[0] in "qk":
                m = WQ if what[0] == "q" else WK
                b, h = what[1] // 2, what[1] % 2
                first = b * S + what[2] * GT
                for c in range(DC):
                    last = mm3(nc, ps, [w_t[:, m, w, c, h * DH:(h + 1) * DH] for w in (HI, LO)],
                               [tok_t[:, w, c, first:first + GT] for w in (HI, LO)], c == 0, c == DC - 1)
            else:
                for k in range(2):
                    first = what[1] * S + (2 * what[2] + k) * P
                    for c in range(DC):
                        last = mm3(nc, ps[:, k * 2 * DH:(k + 1) * 2 * DH],
                                   [tok_t[:, w, c, first:first + P] for w in (HI, LO)],
                                   [w_t[:, WV, w, c, :] for w in (HI, LO)], c == 0, c == DC - 1)
            last.then_inc(item_done, 1)

        def step(hp, u, nxt):
            f = of_unit(hp, u, 0)
            if f:
                a, s, i = f
                n = unit(a, s, i)
                if not (is_first(a) and u < 2):
                    pe.wait_ge(b_done, n - 1)
                if i in (0, QG):
                    half = 0 if i == 0 else 1
                    if s > 0:
                        pe.wait_ge(ilo_done, number(a, ("k", s, half), nxt))
                    elif is_first(a):
                        pe.wait_ge(ilo_done, START.index(("k", 0, half)) + 1)
                    else:
                        pe.wait_ge(ilo_done, number(a - 1, ("k", s, half)))
                ps, o = psum[u % 2], at_s(i)
                k = 0
                while k < width(i):
                    m = min(width(i) - k, 512 - (o + k) % 512)
                    last = mm3(nc, ps[:, o + k:o + k + m],
                               [q_t[:, s % 2, w, i * P:(i + 1) * P] for w in (HI, LO)],
                               [k_t[:, s % 2, w, k:k + m] for w in (HI, LO)], True, True)
                    k += m
                last.then_inc(s_done, 1)
            f = of_unit(hp, u, LAG)
            if f:
                a, s, i = f
                pe.wait_ge(norm_done, unit(a, s, i) + 1)
                for n, tiles in enumerate(turn_banks(i)):
                    at = turn_number(a, s, i, n)
                    if not (is_first(a) and at < 2):
                        pe.wait_ge(tlo_done, at - 1)
                    for t in tiles:
                        last = nc.tensor.transpose(
                            turn_ps[turn_slot(s, i, n)][:, (t - tiles[0]) * P:(t - tiles[0] + 1) * P],
                            prob_of(i)[:, t * P:(t + 1) * P], ident[:, :])
                    last.then_inc(t_done, 1)
            for a, s, g, tiles, first, final in pieces(hp, u):
                if first:
                    n = 2 * ST * a + 2 * s + g
                    if not (is_first(a) and n == 0):
                        pe.wait_ge(z_done, n)
                    i = QG * g + QG - 1
                    pe.wait_ge(tlo_done, turn_number(a, s, i, len(turn_banks(i)) - 1) + 1)
                for t in tiles:
                    if first and t == 0 and g == 0 and s % 2 == 0:
                        if is_first(a) and s == 0:
                            pe.wait_ge(ilo_done, NS)
                        elif s == 0:
                            pe.wait_ge(ilo_done, number(a - 1, ("v", 0, 3)))
                        else:
                            pe.wait_ge(ilo_done, number(a, ("v", 1, 3), nxt))
                    q = max(0, t - QG * g) * P
                    last = mm3(nc, z_ps[:, q:GT],
                               [v[:, s // 2, w, t, s % 2 * DH:(s % 2 + 1) * DH] for w in (HI, LO)],
                               [p_t[g][:, w, t, q:GT] for w in (HI, LO)],
                               t == 0, final and t == tiles[-1])
                if final:
                    last.then_inc(pv_done, 1)
            for n, what in item_at(hp, u, nxt):
                if what == ("w", WV):
                    pe.wait_ge(w_in, 16 * 3 * (hp + 2))
                if what[0] == "o":
                    pe.wait_ge(wo_in[what[1] % 3], 16 * (what[1] // 3 + 1))
                pe.wait_ge(ilo_done, n)
                item(n, what, item_ps)

        for n, what in enumerate(START):
            if n >= 4:
                pe.wait_ge(ilo_done, n - 3)
            item(n, what, bank[4 + n % 4])
        run(pe, step)

    @block.scalar
    def _(act):
        def item_hi(n, what, ps):
            act.wait_ge(item_done, n + 1)
            nc.scalar.activation(places(what, HI), ps, ACT.Copy, scale=scale_of(what)).then_inc(ihi_done, 1)

        for n, what in enumerate(START):
            item_hi(n, what, bank[4 + n % 4])

        def step(hp, u, nxt):
            f = of_unit(hp, u, 1)
            if f:
                a, s, i = f
                n = unit(a, s, i)
                act.wait_ge(b_done, n + 1)
                nc.scalar.activation(prob_of(i), prob_of(i), ACT.Exp, scale=-1.0,
                                     bias=minus_max[:, i:i + 1], accum_out=row_sum[:, i:i + 1])\
                    .then_inc(exp_done, 1)
            f = of_unit(hp, u, LAG)
            if f:
                a, s, i = f
                if i % QG == 0 and not (is_first(a) and s == 0):
                    act.wait_ge(pv_done, 2 * ST * a + 2 * s + i // QG - 1)
                for n, tiles in enumerate(turn_banks(i)):
                    act.wait_ge(t_done, turn_number(a, s, i, n) + 1)
                    nc.scalar.activation(turned_place(s, i, n, HI),
                                         turn_ps[turn_slot(s, i, n)][:, 0:len(tiles) * P]
                                         .rearrange("p (t q) -> p t q", q=P), ACT.Copy)\
                        .then_inc(thi_done, 1)
            for a, s, g, _, _, final in pieces(hp, u - 1):
                if final:
                    n = 2 * ST * a + 2 * s + g
                    act.wait_ge(pv_done, n + 1)
                    if not (is_first(a) and n < 2):
                        act.wait_ge(z_out[g], 16 * (ST * a + s))
                    nc.scalar.activation(z_sb[:, g, :], z_ps, ACT.Copy).then_inc(z_done, 1)
            for n, what in item_at(hp, u, nxt):
                item_hi(n, what, item_ps)
        run(act, step)

    @block.vector
    def _(dve):
        def item_lo(n, what, ps):
            dve.wait_ge(ihi_done, n + 1)
            nc.vector.scalar_tensor_tensor(places(what, LO), ps, scale_of(what),
                                           places(what, HI).bitcast(F32), ALU.mult, ALU.subtract)\
                .then_inc(ilo_done, 1)

        for n, what in enumerate(START):
            item_lo(n, what, bank[4 + n % 4])

        def step(hp, u, nxt):
            g = of_unit(hp, u, LAG + 1)
            if g:
                ga, gs, gi = g
                for k, tiles in enumerate(turn_banks(gi)):
                    dve.wait_ge(thi_done, turn_number(ga, gs, gi, k) + 1)
                    nc.vector.tensor_tensor(turned_place(gs, gi, k, LO),
                                            turn_ps[turn_slot(gs, gi, k)][:, 0:len(tiles) * P]
                                            .rearrange("p (t q) -> p t q", q=P),
                                            turned_place(gs, gi, k, HI).bitcast(F32), ALU.subtract)\
                        .then_inc(tlo_done, 1)
            for k, what in item_at(hp, u - 1, nxt) if u >= 1 else item_before(hp):
                item_lo(k, what, item_ps)
            f = of_unit(hp, u, 0)
            if f:
                a, s, i = f
                n = unit(a, s, i)
                o = at_s(i)
                ps = psum[u % 2][:, o:o + width(i)]
                dve.wait_ge(s_done, n + 1)
                nc.vector.tensor_scalar(ps, ps, CLIP, -CLIP, ALU.min, ALU.max).then_inc(clip_done, 1)
            g = of_unit(hp, u, 1)
            if g:
                ga, gs, gi = g
                dve.wait_ge(exp_done, unit(ga, gs, gi) + 1)
                nc.vector.reciprocal(inv_sum[:, gi:gi + 1], row_sum[:, gi:gi + 1]).then_inc(inv_done, 1)
            if f:
                dve.wait_ge(clip_done, n + 1)
                if u >= QT or not is_first(a):
                    t = of_unit(hp, u, QT)
                    dve.wait_ge(t_done, turn_number(*t, len(turn_banks(t[2])) - 1) + 1)
                if i == 0 and s < 2 and not is_first(a):
                    dve.wait_ge(halved, 2 * a - 1 + s)
                dve.sem_inc(dve_taken, 1)
                nc.vector.tensor_tensor_reduce(out=prob_of(i), in0=ps,
                                               in1=bias[:, s % 2, S - width(i):S], scale=-1.0,
                                               scalar=3e38, op0=ALU.add, op1=ALU.min,
                                               accum_out=minus_max[:, i:i + 1]).then_inc(b_done, 1)

        def item_before(hp):
            return [] if is_first(hp) else item_at(hp - 1, NU - 1, True)
        run(dve, step)


def tables():
    had = np.array([[1.0]])
    while had.shape[0] < P:
        had = np.block([[had, had], [had, -had]])
    first = 2.0 ** (-(2.0 ** -(np.log2(H) - 3)))
    column = np.arange(S) - (S - P)
    rows = np.where(column[None, :] > np.arange(P)[:, None], MASKED, column[None, :].astype(np.float64))
    slopes = np.array([first, first * first]).astype(np.float32)
    bias = np.stack([rows * slopes[0], rows * slopes[1]], 1)
    return (np.eye(P, dtype=np.float32), np.stack([had, -had], 1).astype(np.float32),
            bias.astype(np.float32))


_INS = ["L0_attn_resid_pre", "L0_attn_Wq", "L0_attn_Wk", "L0_attn_Wv", "L0_attn_Wo", "L0_ffn_SU_ug",
        "L0_ffn_SU_dp", "L0_ffn_Wscale_ug", "L0_ffn_Wscale_dp", "L0_ffn_W_up", "L0_ffn_W_gate",
        "L0_ffn_W_down"]


def kernel(**inputs):
    import concourse.bacc as bacc
    from concourse.bass_utils import run_bass_kernel_spmd

    nc = bacc.Bacc("TRN2", target_bir_lowering=False, num_devices=1)
    arrays, args = {}, []
    named = [(n, np.ascontiguousarray(inputs[n])) for n in _INS]
    named += list(zip(["c_ident", "c_had", "c_bias"], tables()))
    for name, a in named:
        arrays[f"in_{name}"] = a
        args.append(nc.dram_tensor(f"in_{name}", a.shape, F32, kind="ExternalInput").ap())
    out = nc.dram_tensor("out", [B, S, D], F32, kind="ExternalOutput").ap()
    build(nc, *args, out)
    r = run_bass_kernel_spmd(nc, [arrays], core_ids=[0])
    return r.results[0]["out"]
```
